# Optimizing a Trainium2 kernel written in Bass

```python
import numpy as np
import jax
import jax.numpy as jnp

def _softmax(x, axis=-1):
    return jax.nn.softmax(x, axis=axis)
def _gelu(x):
    return jax.nn.gelu(x, approximate=True)
def _silu(x):
    return jax.nn.silu(x)
def _sigmoid(x):
    return jax.nn.sigmoid(x)
def _layernorm(x, axis=-1, eps=1e-5):
    m = jnp.mean(x, axis=axis, keepdims=True)
    v = jnp.var(x, axis=axis, keepdims=True)
    return (x - m) / jnp.sqrt(v + eps)
def _scatter_add(tgt, idx, src, axis=0):
    return tgt.at[idx].add(src)
def _segment_sum(src, seg, n):
    return jax.ops.segment_sum(src, seg, n)

kernel_name = 'mk_conv_preact_d2_conv_nchw256_cce28f'

def setup_inputs(seed: int = 0):
    np.random.seed(seed)
    _w = jnp.asarray
    def _rec_inputs():
        import jax
        import jax.numpy as jnp
        _gk = jax.random.key(seed)
        x = -0.0003929 + 0.9999 * jax.random.normal(jax.random.fold_in(_gk, 1), (4, 256, 128, 128), jnp.float32)
        return x
    x = _rec_inputs()
    def _L0_conv_setup():
        import jax, jax.numpy as jnp
        import numpy as np
        GROUP = 256
        K = 3
        EPS = 1e-05
        key = jax.random.key(seed)
        k1, k2 = jax.random.split(key, 2)
        n, c, h, w = (4, 256, 128, 128)
        Ck = c // GROUP
        oc = Ck * K * K
        x = jax.random.normal(k1, (n, c, h, w), jnp.float32)
        w_conv = jax.random.normal(k2, (oc, c), jnp.float32) * 0.02
        gamma = jnp.ones((oc,), jnp.float32)
        beta = jnp.zeros((oc,), jnp.float32)
        return {'x': x, 'w_conv': w_conv, 'gamma': gamma, 'beta': beta}
    _L0_conv_all = _L0_conv_setup()
    _L0_conv_in = {k: v for k, v in _L0_conv_all.items() if k in ('w_conv', 'gamma', 'beta', )}
    del _L0_conv_all

    def _L1_conv_setup():
        import jax, jax.numpy as jnp
        from jax import lax
        import numpy as np
        B_, C_, H_, W_ = (4, 256, 64, 64)
        DM = C_ // 4
        DI = 2 * DM
        NS = 16
        KC = 4
        RK = max(1, DM // 16)
        EPS = 1e-05

        def layernorm(x, g, b):
            m = jnp.mean(x, -1, keepdims=True)
            v = jnp.mean(jnp.square(x - m), -1, keepdims=True)
            return (x - m) * lax.rsqrt(v + EPS) * g + b

        def mamba(x, W_in, W_conv, b_conv, W_xproj, W_dt, b_dt, A_log, D_par, W_outp):
            Bt, L, _ = x.shape
            xz = x @ W_in.T
            xc, z = (xz[..., :DI], xz[..., DI:])
            xt = jnp.transpose(xc, (0, 2, 1))
            xt = lax.conv_general_dilated(xt, W_conv, (1,), [(KC - 1, 0)], feature_group_count=DI)
            xc = jax.nn.silu(jnp.transpose(xt + b_conv[None, :, None], (0, 2, 1)))
            x_dbl = xc @ W_xproj.T
            dt = jax.nn.softplus(x_dbl[..., :RK] @ W_dt.T + b_dt)
            Bm = x_dbl[..., RK:RK + NS]
            Cm = x_dbl[..., RK + NS:]
            A = -jnp.exp(A_log)
            a = jnp.exp(dt[..., None] * A)
            bx = dt[..., None] * Bm[:, :, None, :] * xc[..., None]

            def step(h, inp):
                a_t, b_t, c_t = inp
                h = a_t * h + b_t
                y = jnp.einsum('bdn,bn->bd', h, c_t)
                return (h, y)
            h0 = jnp.zeros((Bt, DI, NS), x.dtype)
            _, ys = lax.scan(step, h0, (jnp.swapaxes(a, 0, 1), jnp.swapaxes(bx, 0, 1), jnp.swapaxes(Cm, 0, 1)))
            y = jnp.swapaxes(ys, 0, 1) + xc * D_par
            y = y * jax.nn.silu(z)
            return y @ W_outp.T
        key = jax.random.key(seed)
        ks = jax.random.split(key, 16)
        r = lambda i, shape, s=0.02: jax.random.normal(ks[i], shape, jnp.float32) * s
        return dict(x=jax.random.normal(ks[0], (B_, C_, H_, W_), jnp.float32), g_norm=jnp.ones((C_,), jnp.float32), b_norm=jnp.zeros((C_,), jnp.float32), g_norm1=jnp.ones((DM,), jnp.float32), b_norm1=jnp.zeros((DM,), jnp.float32), W_in=r(1, (2 * DI, DM)), W_conv=r(2, (DI, 1, KC), 0.1), b_conv=r(3, (DI,)), W_xproj=r(4, (RK + 2 * NS, DI)), W_dt=r(5, (DI, RK), 0.1), b_dt=r(6, (DI,)), A_log=jnp.tile(jnp.log(jnp.arange(1, NS + 1, dtype=jnp.float32)), (DI, 1)), D_par=jnp.ones((DI,), jnp.float32), W_outp=r(7, (DM, DI)), skip_scale=jnp.ones((1,), jnp.float32), W_fc1=r(8, (4 * DM, DM)), b_fc1=jnp.zeros((4 * DM,), jnp.float32), W_fc2=r(9, (DM, 4 * DM)), b_fc2=jnp.zeros((DM,), jnp.float32), W_out=r(10, (C_, C_)), bn_g=jnp.ones((C_,), jnp.float32), bn_b=jnp.zeros((C_,), jnp.float32), bn_mean=jnp.zeros((C_,), jnp.float32), bn_var=jnp.ones((C_,), jnp.float32))
    _L1_conv_all = _L1_conv_setup()
    _L1_conv_in = {k: v for k, v in _L1_conv_all.items() if k in ('g_norm', 'b_norm', 'g_norm1', 'b_norm1', 'W_in', 'W_conv', 'b_conv', 'W_xproj', 'W_dt', 'b_dt', 'A_log', 'D_par', 'W_outp', 'skip_scale', 'W_fc1', 'b_fc1', 'W_fc2', 'b_fc2', 'W_out', 'bn_g', 'bn_b', 'bn_mean', 'bn_var', )}
    del _L1_conv_all

    return {
        "x": x,
        "L0_conv_w_conv": _L0_conv_in["w_conv"],
        "L0_conv_gamma": _L0_conv_in["gamma"],
        "L0_conv_beta": _L0_conv_in["beta"],
        "L1_conv_g_norm": _L1_conv_in["g_norm"],
        "L1_conv_b_norm": _L1_conv_in["b_norm"],
        "L1_conv_g_norm1": _L1_conv_in["g_norm1"],
        "L1_conv_b_norm1": _L1_conv_in["b_norm1"],
        "L1_conv_W_in": _L1_conv_in["W_in"],
        "L1_conv_W_conv": _L1_conv_in["W_conv"],
        "L1_conv_b_conv": _L1_conv_in["b_conv"],
        "L1_conv_W_xproj": _L1_conv_in["W_xproj"],
        "L1_conv_W_dt": _L1_conv_in["W_dt"],
        "L1_conv_b_dt": _L1_conv_in["b_dt"],
        "L1_conv_A_log": _L1_conv_in["A_log"],
        "L1_conv_D_par": _L1_conv_in["D_par"],
        "L1_conv_W_outp": _L1_conv_in["W_outp"],
        "L1_conv_skip_scale": _L1_conv_in["skip_scale"],
        "L1_conv_W_fc1": _L1_conv_in["W_fc1"],
        "L1_conv_b_fc1": _L1_conv_in["b_fc1"],
        "L1_conv_W_fc2": _L1_conv_in["W_fc2"],
        "L1_conv_b_fc2": _L1_conv_in["b_fc2"],
        "L1_conv_W_out": _L1_conv_in["W_out"],
        "L1_conv_bn_g": _L1_conv_in["bn_g"],
        "L1_conv_bn_b": _L1_conv_in["bn_b"],
        "L1_conv_bn_mean": _L1_conv_in["bn_mean"],
        "L1_conv_bn_var": _L1_conv_in["bn_var"],
    }

def reference(x, L0_conv_w_conv, L0_conv_gamma, L0_conv_beta, L1_conv_g_norm, L1_conv_b_norm, L1_conv_g_norm1, L1_conv_b_norm1, L1_conv_W_in, L1_conv_W_conv, L1_conv_b_conv, L1_conv_W_xproj, L1_conv_W_dt, L1_conv_b_dt, L1_conv_A_log, L1_conv_D_par, L1_conv_W_outp, L1_conv_skip_scale, L1_conv_W_fc1, L1_conv_b_fc1, L1_conv_W_fc2, L1_conv_b_fc2, L1_conv_W_out, L1_conv_bn_g, L1_conv_bn_b, L1_conv_bn_mean, L1_conv_bn_var):
    import jax
    import jax.numpy as jnp
    def _L0_conv_ref(x, w_conv, gamma, beta):
        import jax, jax.numpy as jnp
        import numpy as np
        GROUP = 256
        K = 3
        EPS = 1e-05
        n, c, h, w = x.shape
        Ck = c // GROUP
        kk = K * K
        xp = x.reshape(n, c, 16, h // 16, 16, w // 16).mean(axis=(3, 5))
        sigma = jnp.einsum('oc,nchw->nohw', w_conv, xp)
        mu = sigma.mean(axis=(0, 2, 3), keepdims=True)
        var = sigma.var(axis=(0, 2, 3), keepdims=True)
        sigma = (sigma - mu) * jax.lax.rsqrt(var + EPS) * gamma[None, :, None, None] + beta[None, :, None, None]
        xpad = jnp.pad(x, ((0, 0), (0, 0), (1, 1), (1, 1)))
        patches = jnp.stack([xpad[:, :, i:i + h, j:j + w] for i in range(K) for j in range(K)], axis=2)
        xg = patches.reshape(n, GROUP, Ck, kk, h * w)
        sg = sigma.reshape(n, Ck, kk, 16 * 16).transpose(0, 3, 1, 2)
        out = jnp.einsum('ngkps,ngkp->ngks', xg, sg)
        return out.reshape(n, c, h, w)

    def _L1_conv_ref(x, g_norm, b_norm, g_norm1, b_norm1, W_in, W_conv, b_conv, W_xproj, W_dt, b_dt, A_log, D_par, W_outp, skip_scale, W_fc1, b_fc1, W_fc2, b_fc2, W_out, bn_g, bn_b, bn_mean, bn_var):
        import jax, jax.numpy as jnp
        from jax import lax
        import numpy as np
        B_, C_, H_, W_ = (4, 256, 64, 64)
        DM = C_ // 4
        DI = 2 * DM
        NS = 16
        KC = 4
        RK = max(1, DM // 16)
        EPS = 1e-05

        def layernorm(x, g, b):
            m = jnp.mean(x, -1, keepdims=True)
            v = jnp.mean(jnp.square(x - m), -1, keepdims=True)
            return (x - m) * lax.rsqrt(v + EPS) * g + b

        def mamba(x, W_in, W_conv, b_conv, W_xproj, W_dt, b_dt, A_log, D_par, W_outp):
            Bt, L, _ = x.shape
            xz = x @ W_in.T
            xc, z = (xz[..., :DI], xz[..., DI:])
            xt = jnp.transpose(xc, (0, 2, 1))
            xt = lax.conv_general_dilated(xt, W_conv, (1,), [(KC - 1, 0)], feature_group_count=DI)
            xc = jax.nn.silu(jnp.transpose(xt + b_conv[None, :, None], (0, 2, 1)))
            x_dbl = xc @ W_xproj.T
            dt = jax.nn.softplus(x_dbl[..., :RK] @ W_dt.T + b_dt)
            Bm = x_dbl[..., RK:RK + NS]
            Cm = x_dbl[..., RK + NS:]
            A = -jnp.exp(A_log)
            a = jnp.exp(dt[..., None] * A)
            bx = dt[..., None] * Bm[:, :, None, :] * xc[..., None]

            def step(h, inp):
                a_t, b_t, c_t = inp
                h = a_t * h + b_t
                y = jnp.einsum('bdn,bn->bd', h, c_t)
                return (h, y)
            h0 = jnp.zeros((Bt, DI, NS), x.dtype)
            _, ys = lax.scan(step, h0, (jnp.swapaxes(a, 0, 1), jnp.swapaxes(bx, 0, 1), jnp.swapaxes(Cm, 0, 1)))
            y = jnp.swapaxes(ys, 0, 1) + xc * D_par
            y = y * jax.nn.silu(z)
            return y @ W_outp.T
        B, C, H, W = x.shape
        L = H * W
        x_flat = jnp.transpose(x.reshape(B, C, L), (0, 2, 1))
        x_norm = layernorm(x_flat, g_norm, b_norm)
        chunks = x_norm.reshape(B, L, 4, DM)
        xs = jnp.transpose(chunks, (2, 0, 1, 3)).reshape(4 * B, L, DM)
        ym = mamba(xs, W_in, W_conv, b_conv, W_xproj, W_dt, b_dt, A_log, D_par, W_outp)
        yn = layernorm(ym, g_norm1, b_norm1)
        yn = jax.nn.gelu(yn @ W_fc1.T + b_fc1, approximate=False) @ W_fc2.T + b_fc2
        ym = yn + skip_scale * xs
        ym = ym.reshape(4, B, L, DM)
        xi = jnp.transpose(ym, (1, 3, 0, 2)).reshape(B, C, H, W)
        y = jnp.einsum('bchw,oc->bohw', xi, W_out)
        scale = bn_g * lax.rsqrt(bn_var + EPS)
        y = y * scale[None, :, None, None] + (bn_b - bn_mean * scale)[None, :, None, None]
        return jax.nn.silu(y)

    def _gn(v, G=32, eps=1e-5):
        B_, C_, H_, W_ = v.shape
        g = v.reshape(B_, G, C_ // G, H_, W_)
        m = jnp.mean(g, axis=(2, 3, 4), keepdims=True)
        s = jnp.var(g, axis=(2, 3, 4), keepdims=True)
        return ((g - m) / jnp.sqrt(s + eps)).reshape(v.shape)

    def _ln_c(v, eps=1e-6):
        m = jnp.mean(v, axis=1, keepdims=True)
        s = jnp.var(v, axis=1, keepdims=True)
        return (v - m) / jnp.sqrt(s + eps)

    def _ln_t(v, eps=1e-5):
        m = jnp.mean(v, axis=-1, keepdims=True)
        s = jnp.var(v, axis=-1, keepdims=True)
        return (v - m) / jnp.sqrt(s + eps)

    def _to_tokens(v):
        B_, C_, H_, W_ = v.shape
        return v.reshape(B_, C_, H_ * W_).transpose(0, 2, 1)
    def _from_tokens(t, like):
        B_, C_, H_, W_ = like.shape
        return t.transpose(0, 2, 1).reshape(B_, C_, H_, W_)

    x = x + _L0_conv_ref(_gn(x), L0_conv_w_conv, L0_conv_gamma, L0_conv_beta)
    x = x + _L1_conv_ref(_gn(x), L1_conv_g_norm, L1_conv_b_norm, L1_conv_g_norm1, L1_conv_b_norm1, L1_conv_W_in, L1_conv_W_conv, L1_conv_b_conv, L1_conv_W_xproj, L1_conv_W_dt, L1_conv_b_dt, L1_conv_A_log, L1_conv_D_par, L1_conv_W_outp, L1_conv_skip_scale, L1_conv_W_fc1, L1_conv_b_fc1, L1_conv_W_fc2, L1_conv_b_fc2, L1_conv_W_out, L1_conv_bn_g, L1_conv_bn_b, L1_conv_bn_mean, L1_conv_bn_var)
    return x


_drawn_inputs = setup_inputs


def setup_inputs(seed=0):
    import zlib

    import numpy as np

    out = dict(_drawn_inputs(seed))
    spreads = {'L0_conv_gamma': (1.0, 0.2),
     'L0_conv_beta': (0.0, 0.1),
     'L1_conv_g_norm': (1.0, 0.6),
     'L1_conv_b_norm': (0.0, 0.8),
     'L1_conv_g_norm1': (1.0, 0.6),
     'L1_conv_b_norm1': (0.0, 0.8),
     'L1_conv_D_par': (1.0, 0.6),
     'L1_conv_b_fc1': (0.0, 0.8),
     'L1_conv_b_fc2': (0.0, 0.8),
     'L1_conv_bn_g': (1.0, 0.6),
     'L1_conv_bn_b': (0.0, 0.53),
     'L1_conv_bn_mean': (0.0, 0.456),
     'L1_conv_bn_var': (1.0, 0.6)}
    factors = {'L1_conv_W_in': 8.0,
     'L1_conv_W_conv': 8.0,
     'L1_conv_b_conv': 8.0,
     'L1_conv_W_xproj': 8.0,
     'L1_conv_W_dt': 8.0,
     'L1_conv_b_dt': 31.798,
     'L1_conv_A_log': 8.0,
     'L1_conv_W_outp': 8.0,
     'L1_conv_W_fc1': 8.0,
     'L1_conv_W_fc2': 8.0}
    for name, (base, spread) in spreads.items():
        noise = np.random.default_rng([zlib.crc32(name.encode()), seed]).standard_normal(out[name].shape)
        drawn = base * np.exp(spread * noise) if base else spread * noise
        out[name] = jnp.asarray(drawn.astype(out[name].dtype))
    for name, factor in factors.items():
        out[name] = (out[name] * factor).astype(out[name].dtype)
    return out
```

```python
from contextlib import ExitStack

import concourse.bass as bass
from concourse import mybir

F32 = mybir.dt.float32
BF16 = mybir.dt.bfloat16
ALU = mybir.AluOpType
ACT = mybir.ActivationFunctionType
AX = mybir.AxisListType

NB, CH, HH, WW = 4, 256, 128, 128
HW = HH * WW
P = 128
NJ = CH // P
NI = NB * NJ
KK = 9
EPS = 1e-5
DM, DI, NS, KC, RK = 64, 128, 16, 4, 4
T = 512
NU = NB * HW // T
UPB = HW // T
NQ = 2 * NS
PX = 2048
NP = HW // PX
PR = PX // WW
PE_TAPS = (0, 1, 2, 3)
DVE_TAPS = (4, 5, 6, 7, 8)
RING = 4
EXP_LN = "natural_log_exp_and_others"

S_HAT, S_MEAN, S_CEN, S_SQ, S_VAR, S_RSTD, S_XN = 0, 1, 2, 3, 4, 5, 6
S_Z, S_ZC, S_CONV0, S_CONV1, S_SILU = 7, 8, 9, 10, 12
S_DT, S_DTV, S_DTE, S_DTU, S_BC, S_BCH, S_BCR, S_BCM, S_BCL = 14, 15, 16, 17, 17, 18, 19, 20, 21
S_OUTP, S_YMC, S_YSQ, S_YVAR, S_YRSTD, S_YN = 6, 7, 8, 9, 10, 11
S_FC1A, S_FC1C, S_FC1B, S_GELU, S_FC2, S_XI, S_XK = 22, 23, 24, 25, 27, 28, 29
S_WOUT, S_FIN, S_RES = 29, 30, 31
S_YEND = 3
LAG = 3


def build(nc, x, w_conv, gamma, beta, g_norm, b_norm, g_norm1, b_norm1, W_inT, W_cv, b_conv, W_xp, W_xpT, W_dtT,
          b_dt, A_log, D_par, W_outpT, skip, W_fc1T, b_fc1, W_fc2T, b_fc2, W_outT, bn_g, bn_b, bn_m, bn_v, out):
    with ExitStack() as ctx:
        def sb(name, shape, dt=F32):
            return ctx.enter_context(nc.sbuf_tensor(name, shape, dt))

        def sem(name):
            return ctx.enter_context(nc.semaphore(name))

        PS = ctx.enter_context(nc.psum_tensor("PS", [P, 8, 512], F32))
        x1s = nc.dram_tensor("x1_scratch", (NU, P, NJ, T), F32, kind="Internal").ap()

        XR0, XR1 = 18 * WW, 18 * 130
        arena = sb("arena", [P, 13824])
        xa = [arena[:, i * PX:(i + 1) * PX] for i in range(4)]
        xb = [arena[:, i * XR0:(i + 1) * XR0].rearrange("p (r c) -> p r c", c=WW) for i in range(2)]
        o = 2 * XR0
        xh = [arena[:, o + i * XR1:o + (i + 1) * XR1].rearrange("p (r c) -> p r c", c=130) for i in range(2)]
        o += 2 * XR1
        x1t = [arena[:, o + i * PX:o + (i + 1) * PX] for i in range(2)]
        assert o + 2 * PX <= 13824

        def ring(k):
            return arena[:, k * RING * T:(k + 1) * RING * T].rearrange("p (r t) -> p r t", t=T)
        decay, drive, hst, csb, prod = [ring(k) for k in range(5)]
        o = 5 * RING * T
        xres = arena[:, o:o + 2 * T]
        ob = arena[:, o + 2 * T:o + 4 * T]
        gel = arena[:, o + 4 * T:o + 6 * T]
        assert o + 6 * T <= 13824

        ident = sb("ident", [P, P])
        grp8 = sb("grp8", [P, P])
        ones = sb("ones", [P, P])
        mean256 = sb("mean256", [P, P])
        half64 = sb("half64", [P, P])
        sel = sb("sel", [3 * 2 * NS, 2 * NS, P], BF16)
        zrow = sb("zrow", [P, 130])
        wcT = sb("wcT", [P, NJ, KK])
        gam = sb("gam", [P, KK])
        bet = sb("bet", [P, KK])
        cvr = sb("cvr", [P, KC, P])
        wconv = sb("wconv", [P, KC, P])
        win = sb("win", [P, 2 * DI])
        wxp = sb("wxp", [RK, P])
        wdt = sb("wdt", [RK, P])
        wdx = sb("wdx", [P, P])
        wbc = sb("wbc", [P, 3 * 2 * NS])
        wop = sb("wop", [P, DM])
        wsum = sb("wsum", [P, 1])
        wfc1r = sb("wfc1r", [P, 4 * DM])
        wfc1 = sb("wfc1", [P, 4 * DM])
        wfc2 = sb("wfc2", [P, 2, DM])
        wout = sb("wout", [P, NJ, CH])
        cols = sb("cols", [P, 40])
        (c_bconv, c_bdt, c_D, c_skip, c_b2, c_g1, c_b1, c_eps, c_one) = [cols[:, i:i + 1] for i in range(9)]
        c_bfc1, c_gn, c_bn, c_bng, c_bnb, c_bnm, c_bnv = [cols[:, 10 + 2 * i:12 + 2 * i] for i in range(7)]
        c_scale, c_shift, c_tmp = [cols[:, 24 + 2 * i:26 + 2 * i] for i in range(3)]
        c_bf = cols[:, 30:32]
        aneg = sb("aneg", [P, NS])
        keep = sb("keep", [P, NU])
        keepc = sb("keepc", [P, 1])
        pooled = sb("pooled", [P, NI, 256])
        bnst = sb("bnst", [P, 32, 6])
        mvt = sb("mvt", [P, 2])
        mv = sb("mv", [P, NI, 2])
        st = sb("st", [P, 8, NI])
        coef = sb("coef", [P, 2, NI])
        coefU = sb("coefU", [P, NU, 4])
        sg = sb("sg", [P, NI, KK])
        sgd = sb("sgd", [P, NI, KK])
        sq9 = sb("sq9", [P, NI, KK])
        s9 = sb("s9", [P, 4, KK])
        w9 = sb("w9", [P, NI * KK])
        dgw = sb("dgw", [P, 2, len(PE_TAPS), P])

        init = sb("init", [P, 4 * NS])
        xl = sb("xl", [P, 2 * T])
        xhat = sb("xhat", [P, NJ, T])
        sq = sb("sq", [P, NJ, T])
        rstd = sb("rstd", [P, T])
        xn = sb("xn", [P, NJ, 3 + T])
        xk = sb("xk", [P, NJ, T])
        xi = sb("xi", [P, NJ, T])
        xc = sb("xc", [P, 2, 2 * T])
        sz = sb("sz", [P, 2, 2 * T])
        dt = sb("dt", [P, 2, 2 * T])
        du = sb("du", [P, 2, 2 * T])
        rlu = sb("rlu", [P, 2 * T])
        vab = sb("vab", [P, 2 * T])
        res3 = sb("res3", [DM, 2 * T])
        spl = sb("spl", [3 * 2 * NS, 2, 2 * T], BF16)
        ytmp = sb("ytmp", [P, T])
        yz = sb("yz", [P, 2, T])
        ymc = sb("ymc", [P, T])
        ysq = sb("ysq", [P, T])
        yrs = sb("yrs", [P, T])
        yn = sb("yn", [P, T])
        gel1 = sb("gel1", [P, 2 * T])

        s_w = sem("weights_loaded")
        s_cst = sem("constants_made")
        s_za = sem("fill_done")
        s_aload = [sem(f"a_loaded{i}") for i in range(4)]
        s_aused = sem("a_used")
        s_dv = sem("dve_step")
        s_gp = sem("gn_to_pe")
        s_pg = sem("pe_to_gn")
        s_ga = sem("gn_to_act")
        s_ag = sem("act_to_gn")
        s_prep = sem("weights_ready")
        s_an = sem("a_negated")
        s_pp = sem("prep_from_pe")
        s_bload = [sem(f"b_loaded{i}") for i in range(2)]
        s_bused = sem("b_used")
        s_hat = sem("padded_ready")
        s_htap = sem("padded_used_dve")
        s_taps = sem("pe_taps_done")
        s_tapr = sem("pe_taps_read")
        s_diag = sem("diag_ready")
        s_x1 = sem("x1_ready")
        s_st = sem("x1_stored")
        s_x1free = sem("x1_buffer_free")
        u_free = sem("u_result_buffer_free")
        s_bst = sem("b_step")
        s_coef = sem("coefs_ready")
        s_c = sem("stage_c_start")
        s_mv = sem("statistics_kept")
        s_keep = sem("keep_copied")
        q_b, q_c, q_exp, q_cc = sem("q_B_ready"), sem("q_C_ready"), sem("q_decay_ready"), sem("q_C_copied")
        q_drv, q_scan, q_prod, q_sum = sem("q_drive_ready"), sem("q_scanned"), sem("q_product_ready"), sem("q_summed")
        k_y, k_yz = sem("k_y_read"), sem("k_yz_ready")
        u_xl, u_hat, u_mean, u_cen = sem("u_x_loaded"), sem("u_hat"), sem("u_mean"), sem("u_centred")
        u_sq, u_var, u_rstd, u_xg, u_xn = sem("u_sq"), sem("u_var"), sem("u_rstd"), sem("u_xg"), sem("u_xn")
        u_ln, u_hist = sem("u_lnvar"), sem("u_hist")
        u_wout, u_fin, u_res, u_xr, u_out = (sem("u_wout"), sem("u_fin"), sem("u_res"), sem("u_xres_loaded"),
                                             sem("u_stored"))
        p_z, p_zc, p_conv, p_silu = sem("p_z"), sem("p_z_copied"), sem("p_conv"), sem("p_silu")
        p_rl = sem("p_dt_positive")
        p_dt, p_dtv, p_ln, p_e, p_dts, p_u = (sem("p_dt"), sem("p_dt_read"), sem("p_ln"), sem("p_e"), sem("p_dt_sum"),
                                              sem("p_u"))
        p_bc, p_h, p_r, p_m, p_l = sem("p_bc"), sem("p_hi"), sem("p_rest"), sem("p_mid"), sem("p_lo")
        p_op, p_ymc, p_ysq, p_yvar, p_yln, p_yrs, p_yn = [sem(f"p_{n}") for n in
                                                         ("outp", "ymc", "ysq", "yvar", "yln", "yrs", "yn")]
        p_f1a, p_f1c, p_f1b, p_gel, p_f2, p_xi, p_xk = [sem(f"p_{n}") for n in
                                                       ("fc1a", "fc1_copied", "fc1b", "gelu", "fc2", "xi", "xk")]

        xv = x.rearrange("b c h w -> (b c) (h w)")
        xrow = x.rearrange("b c h w -> (b c) h w")
        outv = out.rearrange("b (j p) h w -> b p j (h w)", p=P)
        NW = 27

        block = ctx.enter_context(nc.Block())

        def wait(eng, s, v):
            if isinstance(v, int) and v <= 0:
                return
            eng.wait_ge(s, v)

        @block.sync
        def _(sp):
            loads = [
                (wcT[:, :, :], w_conv.rearrange("(j p) o -> p j o", p=P)),
                (gam[:, :], gamma.rearrange("(a k) -> a k", a=1).to_broadcast([P, KK])),
                (bet[:, :], beta.rearrange("(a k) -> a k", a=1).to_broadcast([P, KK])),
                (win[0:DM, :], W_inT), (win[DM:P, :], W_inT),
                (cvr[:, :, :].rearrange("p k d -> p (k d)"), W_cv.rearrange("(a k) -> a k", a=1).to_broadcast([P, KC * DI])),
                (wxp[:, :], W_xp[0:RK, :]), (wdt[:, :], W_dtT),
                (wbc[:, 0:32], W_xpT[:, RK:]), (wbc[:, 32:64], W_xpT[:, RK:]), (wbc[:, 64:96], W_xpT[:, RK:]),
                (wop[:, :], W_outpT), (wfc1r[0:DM, :], W_fc1T), (wfc1r[DM:P, :], W_fc1T),
                (wfc2[:, :, :], W_fc2T.rearrange("(h p) m -> p h m", p=P)),
                (wout[:, :, :], W_outT.rearrange("(j p) o -> p j o", p=P)),
                (aneg[:, :], A_log),
                (c_skip, skip.rearrange("(a k) -> a k", a=1).to_broadcast([P, 1])),
            ]
            for col, v in ((c_bconv, b_conv), (c_bdt, b_dt), (c_D, D_par)):
                loads.append((col, v.rearrange("(p a) -> p a", a=1)))
            for col, v in ((c_b2, b_fc2), (c_g1, g_norm1), (c_b1, b_norm1)):
                for h in range(2):
                    loads.append((col[DM * h:DM * h + DM, :], v.rearrange("(p a) -> p a", a=1)))
            assert len(loads) == NW
            for col, v in ((c_bfc1, b_fc1), (c_gn, g_norm), (c_bn, b_norm), (c_bng, bn_g), (c_bnb, bn_b),
                           (c_bnm, bn_m), (c_bnv, bn_v)):
                for j in range(2):
                    loads.append((col[:, j:j + 1], v[P * j:P * j + P].rearrange("(p a) -> p a", a=1)))
            for dst, src in loads:
                sp.dma_start(dst, src).then_inc(s_w, 16)
            with sp.Fori(0, NI) as im:
                for k in range(NP):
                    sp.wait_ge(s_aused, im * NP + (k + 1))
                    sp.dma_start(xa[k % 4], xv[bass.ds(im * P, P), k * PX:(k + 1) * PX]).then_inc(s_aload[k % 4], 16)
            sp.wait_ge(s_aused, NI * NP + 4)
            with sp.Fori(0, NB) as b:
                for j in range(NJ):
                    for k in range(NP):
                        lo, hi = (1 if k == 0 else 0), (17 if k == NP - 1 else 18)
                        r0 = k * PR - 1 + lo
                        sp.wait_ge(s_bused, b * (NJ * NP) + (j * NP + k + 1))
                        sp.dma_start(xb[k % 2][:, lo:hi, :],
                                     xrow[bass.ds(b * CH + j * P, P), r0:r0 + hi - lo, :]).then_inc(s_bload[k % 2], 16)
            sp.wait_ge(s_c, 1)
            with sp.Fori(0, NB) as b:
                with sp.Fori(0, UPB) as t:
                    u = sp.snap(b * UPB + t)
                    sp.wait_ge(u_res, u + 1)
                    sp.dma_start(xres.rearrange("p (a j t) -> p a j t", a=1, j=NJ),
                                 x1s[bass.ds(u, 1)].rearrange("u p j t -> p u j t")).then_inc(u_xr, 16)
                    sp.wait_ge(u_res, u + 2)
                    sp.dma_start(outv[bass.ds(b, 1), :, :, bass.ds(t * T, T)].rearrange("b p j t -> p b j t"),
                                 ob.rearrange("p (a j t) -> p a j t", a=1, j=NJ)).then_inc(u_out, 16)
                    sp.wait_ge(u_out, 16 * (u + 1))
                    sp.sem_inc(u_free, 1)

        @block.gpsimd
        def _(pool):
            fills = [(ident, 0.0), (grp8, 1 / 8), (ones, 1.0), (mean256, 1 / CH), (half64, 1 / DM), (sel, 0.0),
                     (zrow, 0.0), (keep, 1.0)]
            for tile, v in fills:
                pool.memset(tile[:], v).then_inc(s_za, 1)
            pool.wait_ge(s_za, len(fills))
            pool.affine_select(out=ident[:, :], in_=ident[:, :], compare_op=ALU.not_equal, fill=1.0, base=0,
                               pattern=[[-1, P]], channel_multiplier=1).then_inc(s_cst, 1)
            k = len(fills)
            for tile, g in ((grp8, 8), (half64, DM)):
                v = tile[:, :].rearrange("p (g e) -> p g e", e=g)
                pool.affine_select(out=v, in_=v, compare_op=ALU.is_ge, fill=0.0, base=0,
                                   pattern=[[-g, P // g], [0, g]], channel_multiplier=1).then_inc(s_za, 1)
                k += 1
                pool.wait_ge(s_za, k)
                pool.affine_select(out=v, in_=v, compare_op=ALU.is_ge, fill=0.0, base=g - 1,
                                   pattern=[[g, P // g], [0, g]], channel_multiplier=-1).then_inc(s_cst, 1)
            for r in range(3):
                pool.affine_select(out=sel[:, :, :], in_=sel[:, :, :], compare_op=ALU.not_equal, fill=1.0,
                                   base=-32 * r, pattern=[[-1, 2 * NS], [0, P]], channel_multiplier=1).then_inc(s_za, 1)
                k += 1
                pool.wait_ge(s_za, k)
            pool.memset(keep[:, UPB - 1:NU:UPB], 0.0).then_inc(s_cst, 1)
            with pool.Fori(0, NB) as b:
                for j in range(NJ):
                    for k in range(NP):
                        pool.wait_ge(s_x1, b * (NJ * NP) + (j * NP + k + 1))
                        pool.dma_start(x1s[bass.ds(b * UPB + k * (PX // T), PX // T), :, j, :].rearrange("u p t -> p u t"),
                                       x1t[k % 2].rearrange("p (u t) -> p u t", t=T)).then_inc(s_st, 16)
                        pool.wait_ge(s_st, b * (16 * NJ * NP) + 16 * (j * NP + k + 1))
                        pool.sem_inc(s_x1free, 1)
            pool.wait_ge(s_coef, 1)
            pool.sem_inc(s_c, 1)

            def unit(u):
                wait(pool, q_prod, u * (2 * NQ))
                pool.sem_inc(s_keep, 1)
                pool.tensor_copy(keepc[:, :], keep[:, bass.ds(u, 1)]).then_inc(s_keep, 1)
                pool.wait_ge(s_keep, 2 * u + 2)
                for q in range(2 * NQ):
                    g = u * (2 * NQ) + q
                    r = q % RING
                    pool.wait_ge(q_scan, g + 1)
                    pool.tensor_tensor(init[:, q:q + 1], hst[:, r, T - 1:T], keepc[:, :],
                                       ALU.mult)
                    pool.wait_ge(q_cc, g + 1)
                    if not (isinstance(u, int) and u == 0 and q < RING):
                        pool.wait_ge(q_sum, g - (RING - 1))
                    pool.tensor_tensor(prod[:, r, :], hst[:, r, :], csb[:, r, :], ALU.mult).then_inc(q_prod, 1)

            unit(0)
            with pool.Fori(1, NU) as u:
                unit(u)

        @block.scalar
        def _(act):
            act.wait_ge(s_w, 16 * (NW + 14))
            act.activation(aneg[:, :], aneg[:, :], ACT.Exp).then_inc(s_an, 1)

            def gn_sqrt(n):
                act.wait_ge(s_ga, n)
                act.activation(st[:, 5, :], st[:, 4, :], ACT.Sqrt).then_inc(s_ag, 1)
            gn_sqrt(1)
            act.wait_ge(s_ga, 2)
            act.activation(s9[:, 2, :], s9[:, 1, :], ACT.Sqrt).then_inc(s_ag, 1)
            act.wait_ge(s_ga, 3)
            act.activation(c_tmp, c_scale, ACT.Sqrt).then_inc(s_ag, 1)
            act.wait_ge(s_ga, 4)
            with act.Fori(0, NB) as b:
                for j in range(NJ):
                    for k in range(NP):
                        n = b * (NJ * NP) + (j * NP + k)
                        lo, hi = (1 if k == 0 else 0), (17 if k == NP - 1 else 18)
                        act.wait_ge(s_bload[k % 2], b * (8 * NJ * NP) + 16 * ((j * NP + k) // 2 + 1))
                        act.wait_ge(s_htap, n + 1)
                        act.wait_ge(s_taps, n + 1)
                        if k == 0:
                            act.activation(xh[0][:, 0, :], zrow[:, :], ACT.Copy)
                        if k == NP - 1:
                            act.activation(xh[1][:, 17, :], zrow[:, :], ACT.Copy)
                        act.sem_inc(s_an, 1)
                        act.activation(xh[k % 2][:, lo:hi, 1:129], xb[k % 2][:, lo:hi, :], ACT.Identity,
                                       bias=coef[:, 1, bass.ds(b * NJ + j, 1)],
                                       scale=coef[:, 0, bass.ds(b * NJ + j, 1)]).then_inc(s_hat, 1)
            gn_sqrt(5)
            act.wait_ge(s_c, 1)
            act.preload_act_table_set(EXP_LN)

            def load_x(u):
                act.dma_start(xl[:, :].rearrange("p (a j t) -> p a j t", a=1, j=NJ),
                              x1s[bass.ds(u, 1)].rearrange("u p j t -> p u j t")).then_inc(u_xl, 16)

            def norm_sq(u):
                act.wait_ge(u_cen, u + 1)
                act.activation(sq[:, :, :], xhat[:, :, :], ACT.Square).then_inc(u_sq, 1)

            def norm_rstd(u):
                act.wait_ge(u_var, u + 1)
                act.activation(rstd[:, :], PS[:, 7, :], ACT.Ln, bias=c_eps).then_inc(u_ln, 1)
                act.wait_ge(u_ln, u + 1)
                act.activation(rstd[:, :], rstd[:, :], ACT.Exp, scale=-0.5).then_inc(u_rstd, 1)

            def silus(u, j):
                s = 2 * u + j
                act.wait_ge(p_zc, s + 1)
                wait(act, k_yz, 2 * s - 2)
                act.activation(sz[:, j, :], sz[:, j, :], ACT.Silu)
                act.wait_ge(p_conv, s + 1)
                act.activation(xc[:, j, :], PS[:, 5:7, :].rearrange("p a t -> p (a t)"), ACT.Silu,
                               bias=c_bconv).then_inc(p_silu, 1)
                act.preload_act_table_set(EXP_LN)

            def dt_exp(u, j):
                s = 2 * u + j
                act.wait_ge(p_dtv, s + 1)
                act.activation(vab[:, :], vab[:, :], ACT.Exp, bias=c_bdt).then_inc(p_e, 1)
                act.wait_ge(p_e, s + 1)
                act.activation(vab[:, :], vab[:, :], ACT.Ln, bias=c_one).then_inc(p_ln, 1)

            def bc_hi(u, j):
                s = 2 * u + j
                act.wait_ge(p_bc, s + 1)
                act.activation(spl[:, j, :], PS[0:96, 5:7, :].rearrange("p a t -> p (a t)"), ACT.Copy).then_inc(p_h, 1)

            def bc_mid(u, j):
                s = 2 * u + j
                act.wait_ge(p_r, s + 1)
                act.activation(spl[0:64, j, :], res3[:, :], ACT.Copy).then_inc(p_m, 1)

            def y_sq(u, j):
                s = 2 * u + j
                act.wait_ge(p_ymc, s + 1)
                act.activation(ysq[:, :], ymc[:, :], ACT.Square).then_inc(p_ysq, 1)

            def y_rstd(u, j):
                s = 2 * u + j
                act.wait_ge(p_yvar, s + 1)
                act.activation(yrs[:, :], PS[:, 7, :], ACT.Ln, bias=c_eps).then_inc(p_yln, 1)
                act.wait_ge(p_yln, s + 1)
                act.activation(yrs[:, :], yrs[:, :], ACT.Exp, scale=-0.5).then_inc(p_yrs, 1)

            def gelus(u, j):
                s = 2 * u + j
                act.wait_ge(p_f1c, s + 1)
                act.activation(gel, gel, ACT.Gelu, bias=c_bf[:, 0:1])
                act.wait_ge(p_f1b, s + 1)
                act.activation(gel1[:, :], PS[:, 5:7, :].rearrange("p a t -> p (a t)"), ACT.Gelu,
                               bias=c_bf[:, 1:2]).then_inc(p_gel, 1)
                act.preload_act_table_set(EXP_LN)

            def skip_path(u, j):
                s = 2 * u + j
                act.wait_ge(u_xn, u + 1)
                wait(act, p_xi, s - 1)
                act.activation(xk[:, j, :], xn[:, j, 3:], ACT.Identity, bias=c_b2, scale=c_skip).then_inc(p_xk, 1)

            def final(u):
                act.wait_ge(u_wout, u + 1)
                for h in range(2):
                    ins = act.activation(xhat_o[:, h, :], PS[:, 5 + h, :], ACT.Silu, bias=c_shift[:, h:h + 1],
                                         scale=c_scale[:, h:h + 1])
                ins.then_inc(u_fin, 1)
                act.preload_act_table_set(EXP_LN)
            xhat_o = sq

            def unit(u, first, last):
                for j in range(2):
                    for q in range(NQ):
                        g = u * (2 * NQ) + (j * NQ + q)
                        r = q % RING
                        n, c = q % NS, q // NS
                        if q == 0:
                            act.wait_ge(p_u, 2 * u + j + 1)
                        if not (first and j == 0 and q < RING):
                            act.wait_ge(q_scan, g - (RING - 1))
                        act.activation(decay[:, r, :], dt[:, j, c * T:(c + 1) * T], ACT.Exp,
                                       scale=aneg[:, n:n + 1]).then_inc(q_exp, 1)
                        act.wait_ge(q_c, g + 1)
                        if not (first and j == 0 and q < RING):
                            act.wait_ge(q_prod, g - (RING - 1))
                        act.activation(csb[:, r, :], PS[:, 2 + q % 2, :], ACT.Copy).then_inc(q_cc, 1)
                        nu, nj = (u, 1) if j == 0 else (u + 1, 0)
                        bu, bj = (u - 1, 1) if j == 0 else (u, 0)
                        front = not (last and j == 1)
                        back = not (first and j == 0)
                        if j == 0 and q == 1 and not last:
                            load_x(u + 1)
                        if j == 1 and not last:
                            if q == S_SQ:
                                norm_sq(nu)
                            if q == S_RSTD:
                                norm_rstd(nu)
                        if front:
                            if q == S_SILU:
                                silus(nu, nj)
                            if q == S_DTE:
                                dt_exp(nu, nj)
                            if q == S_BCH:
                                bc_hi(nu, nj)
                            if q == S_BCM:
                                bc_mid(nu, nj)
                            if q == S_XK:
                                skip_path(nu, nj)
                        if back:
                            if q == S_YSQ:
                                y_sq(bu, bj)
                            if q == S_YRSTD:
                                y_rstd(bu, bj)
                            if q == S_GELU:
                                gelus(bu, bj)
                            if q == S_FIN and j == 0:
                                final(bu)

            load_x(0)
            norm_sq(0)
            norm_rstd(0)
            silus(0, 0)
            dt_exp(0, 0)
            bc_hi(0, 0)
            bc_mid(0, 0)
            skip_path(0, 0)
            unit(0, True, False)
            with act.Fori(1, NU - 1) as u:
                unit(u, False, False)
            unit(NU - 1, False, True)
            y_sq(NU - 1, 1)
            y_rstd(NU - 1, 1)
            gelus(NU - 1, 1)
            final(NU - 1)

        @block.tensor
        def _(pe):
            pe.wait_ge(s_cst, 4)
            pe.wait_ge(s_w, 16 * (NW + 14))
            pe.matmul(PS[:, 4, 0:P], wxp[:, :], wdt[:, :], start=True, stop=True)
            for h in range(2):
                for c in range(2):
                    if c == 0:
                        ins = pe.matmul(PS[:, 5, h:h + 1], wfc1r[0:DM, h * P:(h + 1) * P], c_b1[0:DM, :],
                                        start=(h == 0), stop=True, skip_group_check=True)
            ins.then_inc(s_pp, 1)

            def gn_pe(n):
                pe.wait_ge(s_gp, n)
                pe.matmul(PS[:, 0, 0:NI], grp8[:, :], st[:, 0, :], start=True, stop=True).then_inc(s_pg, 1)
                pe.wait_ge(s_gp, n + 1)
                pe.matmul(PS[:, 1, 0:NI], grp8[:, :], st[:, 3, :], start=True, stop=True).then_inc(s_pg, 1)
            gn_pe(1)
            pe.wait_ge(s_gp, 3)
            for b in range(NB):
                for h in range(2):
                    for j in range(NJ):
                        i = b * 2 + h
                        ins = pe.matmul(PS[:, 2, i * KK:(i + 1) * KK],
                                        pooled[:, b * NJ + j, h * P:(h + 1) * P], wcT[:, j, :],
                                        start=(i == 0 and j == 0), stop=(j == NJ - 1), skip_group_check=True)
            ins.then_inc(s_pg, 1)
            pe.wait_ge(s_gp, 4)
            pe.matmul(PS[:, 3, 0:NI * KK], ones[:, :], sg[:, :, :].rearrange("p g o -> p (g o)"),
                      start=True, stop=True).then_inc(s_pg, 1)
            pe.wait_ge(s_gp, 5)
            pe.matmul(PS[:, 0, 0:NI * KK], ones[:, :], sq9[:, :, :].rearrange("p g o -> p (g o)"),
                      start=True, stop=True).then_inc(s_pg, 1)
            pe.sem_inc(s_taps, 2)
            with pe.Fori(0, NB) as b:
                for j in range(NJ):
                    pe.wait_ge(s_diag, b * NJ + (j + 1))
                    for k in range(NP):
                        n = b * (NJ * NP) + (j * NP + k)
                        pe.wait_ge(s_hat, n + 1)
                        pe.wait_ge(s_tapr, n + 1)
                        for rb in range(4):
                            for i, tap in enumerate(PE_TAPS):
                                dy, dx = tap // 3, tap % 3
                                ins = pe.matmul(PS[:, 4 * (k % 2) + rb, :].rearrange("p (r c) -> p r c", c=WW),
                                                dgw[:, j, i, :],
                                                xh[k % 2][:, 4 * rb + dy:4 * rb + dy + 4, dx:dx + WW],
                                                start=(i == 0), stop=(i == len(PE_TAPS) - 1))
                        ins.then_inc(s_taps, 1)
            gn_pe(6)
            pe.wait_ge(s_c, 1)
            pe.wait_ge(s_prep, 1)

            W = [PS[:, 5, :], PS[:, 6, :]]
            V = PS[:, 7, :]

            def norm_mean(u):
                pe.wait_ge(u_hat, u + 1)
                wait(pe, p_xi, 2 * u - 2)
                pe.matmul(V, mean256[:, :], xhat[:, 0, :], start=True, stop=False)
                pe.matmul(V, mean256[:, :], xhat[:, 1, :], start=False, stop=True).then_inc(u_mean, 1)

            def norm_var(u):
                pe.wait_ge(u_sq, u + 1)
                pe.matmul(V, mean256[:, :], sq[:, 0, :], start=True, stop=False)
                pe.matmul(V, mean256[:, :], sq[:, 1, :], start=False, stop=True).then_inc(u_var, 1)

            def proj_z(u, j):
                pe.wait_ge(u_xn, u + 1)
                if j == 0:
                    wait(pe, u_fin, u - 1)
                else:
                    wait(pe, p_gel, 2 * u - 1)
                for c in range(2):
                    ins = pe.matmul(W[c], win[c * DM:(c + 1) * DM, DI:], xn[c * DM:(c + 1) * DM, j, 3:],
                                    start=True, stop=True)
                ins.then_inc(p_z, 1)

            def conv(u, j, part):
                s = 2 * u + j
                if part == 0:
                    pe.wait_ge(p_zc, s + 1)
                for k in (0, 1) if part == 0 else (2, 3):
                    for c in range(2):
                        ins = pe.matmul(W[c], wconv[c * DM:(c + 1) * DM, k, :],
                                        xn[c * DM:(c + 1) * DM, j, k:k + T],
                                        start=(k == 0), stop=(k == KC - 1))
                if part == 1:
                    ins.then_inc(p_conv, 1)

            def proj_dt(u, j):
                pe.wait_ge(p_silu, 2 * u + j + 1)
                for c in range(2):
                    ins = pe.matmul(W[c], wdx[:, :], xc[:, j, c * T:(c + 1) * T], start=True, stop=True)
                ins.then_inc(p_dt, 1)

            def proj_bc(u, j):
                pe.wait_ge(p_dtv, 2 * u + j + 1)
                for c in range(2):
                    ins = pe.matmul(PS[0:96, 5 + c, :], wbc[:, :], xc[:, j, c * T:(c + 1) * T], start=True, stop=True)
                ins.then_inc(p_bc, 1)

            def out_proj(u, j, front=True):
                s = 2 * u + j
                pe.wait_ge(k_yz, 2 * s + 2)
                wait(pe, p_xi, s)
                if j == 0 and front:
                    pe.wait_ge(u_ln, u + 2)
                for c in range(2):
                    ins = pe.matmul(PS[c * DM:(c + 1) * DM, 7, :], wop[:, :], yz[:, c, :], start=True, stop=True)
                ins.then_inc(p_op, 1)

            def y_var(u, j):
                pe.wait_ge(p_ysq, 2 * u + j + 1)
                pe.matmul(V, half64[:, :], ysq[:, :], start=True, stop=True).then_inc(p_yvar, 1)

            def fc1(u, j, h, front=True):
                s = 2 * u + j
                if h == 0:
                    pe.wait_ge(p_yn, s + 1)
                    if front:
                        pe.wait_ge(p_r, s + 3)
                    elif j == 0:
                        pe.wait_ge(u_fin, u)
                else:
                    pe.wait_ge(p_f1c, s + 1)
                for c in range(2):
                    ins = pe.matmul(W[c], wfc1[c * DM:(c + 1) * DM, h * P:(h + 1) * P], yn[c * DM:(c + 1) * DM, :],
                                    start=True, stop=True)
                ins.then_inc(p_f1a if h == 0 else p_f1b, 1)

            def fc2(u, j):
                pe.wait_ge(p_gel, 2 * u + j + 1)
                for h, g in enumerate((gel, gel1[:, :])):
                    for c in range(2):
                        ins = pe.matmul(PS[c * DM:(c + 1) * DM, 7, :], wfc2[:, h, :], g[:, c * T:(c + 1) * T],
                                        start=(h == 0), stop=(h == 1))
                ins.then_inc(p_f2, 1)

            def w_out(u):
                pe.wait_ge(p_xi, 2 * u + 2)
                for h in range(2):
                    for j in range(NJ):
                        ins = pe.matmul(W[h], wout[:, j, h * P:(h + 1) * P], xi[:, j, :],
                                        start=(j == 0), stop=(j == NJ - 1))
                ins.then_inc(u_wout, 1)

            def bcast(u, j, q, first):
                g = u * (2 * NQ) + (j * NQ + q)
                n, c = q % NS, q // NS
                if q == 0:
                    pe.wait_ge(p_l, 2 * u + j + 1)
                rhs = spl[:, j, c * T:(c + 1) * T]
                early = first and j == 0 and q < 2
                if not early:
                    pe.wait_ge(q_drv, g - 1)
                pe.matmul(PS[:, q % 2, :], sel[:, n, :], rhs, start=True, stop=True).then_inc(q_b, 1)
                if not early:
                    pe.wait_ge(q_cc, g - 1)
                pe.matmul(PS[:, 2 + q % 2, :], sel[:, NS + n, :], rhs, start=True, stop=True).then_inc(q_c, 1)

            def total(u, j, q):
                g = u * (2 * NQ) + (j * NQ + q)
                n, c = q % NS, q // NS
                pe.wait_ge(q_prod, g + 1)
                if n == 0:
                    wait(pe, k_y, (2 * u + j) * 2 + c)
                pe.matmul(PS[:, 4, :], ident[:, :], prod[:, q % RING, :], start=(n == 0),
                          stop=(n == NS - 1), skip_group_check=True).then_inc(q_sum, 1)

            def unit(u, first, last):
                for j in range(2):
                    for q in range(NQ):
                        if q + 1 < NQ:
                            bcast(u, j, q + 1, first)
                        elif j == 0:
                            bcast(u, 1, 0, False)
                        elif not last:
                            bcast(u + 1, 0, 0, False)
                        nu, nj = (u, 1) if j == 0 else (u + 1, 0)
                        bu, bj = (u - 1, 1) if j == 0 else (u, 0)
                        front = not (last and j == 1)
                        back = not (first and j == 0)
                        if j == 1 and not last:
                            if q == S_MEAN:
                                norm_mean(nu)
                            if q == S_VAR:
                                norm_var(nu)
                        if front:
                            if q == S_Z:
                                proj_z(nu, nj)
                            if q == S_CONV0:
                                conv(nu, nj, 0)
                            if q == S_CONV1:
                                conv(nu, nj, 1)
                            if q == S_DT:
                                proj_dt(nu, nj)
                            if q == S_BC:
                                proj_bc(nu, nj)
                        if back:
                            if q == S_OUTP:
                                out_proj(bu, bj, front)
                            if q == S_YVAR:
                                y_var(bu, bj)
                            if q == S_FC1A:
                                fc1(bu, bj, 0, front)
                            if q == S_FC1B:
                                fc1(bu, bj, 1)
                            if q == S_FC2:
                                fc2(bu, bj)
                            if q == S_WOUT and j == 0:
                                w_out(bu)
                        if q >= LAG:
                            total(u, j, q - LAG)
                        elif j == 1:
                            total(u, 0, NQ + q - LAG)
                        elif not first:
                            total(u - 1, 1, NQ + q - LAG)

            norm_mean(0)
            norm_var(0)
            proj_z(0, 0)
            conv(0, 0, 0)
            conv(0, 0, 1)
            proj_dt(0, 0)
            proj_bc(0, 0)
            bcast(0, 0, 0, True)
            unit(0, True, False)
            with pe.Fori(1, NU - 1) as u:
                unit(u, False, False)
            unit(NU - 1, False, True)
            for q in range(NQ - LAG, NQ):
                total(NU - 1, 1, q)
            out_proj(NU - 1, 1, False)
            y_var(NU - 1, 1)
            fc1(NU - 1, 1, 0, False)
            fc1(NU - 1, 1, 1)
            fc2(NU - 1, 1)
            w_out(NU - 1)

        @block.vector
        def _(dve):
            steps = [0]

            def link(ins):
                steps[0] += 1
                ins.then_inc(s_dv, 1)
                dve.wait_ge(s_dv, steps[0])

            link(dve.memset(c_eps, EPS))
            link(dve.memset(c_one, 1.0))
            link(dve.memset(init[:, :], 0.0))
            link(dve.memset(xn[:, :, 0:3], 0.0))
            dve.sem_inc(s_aused, 4)
            with dve.Fori(0, NI) as im:
                for k in range(NP):
                    dve.wait_ge(s_aload[k % 4], im * (16 * NP // 4) + 16 * (k // 4 + 1))
                    for rb in range(2):
                        dve.tensor_reduce(pooled[:, bass.ds(im, 1), k * 32 + 16 * rb:k * 32 + 16 * rb + 16].rearrange(
                                              "p a w -> p (a w)"),
                                          xa[k % 4][:, rb * 1024:(rb + 1) * 1024].rearrange("p (r w c) -> p w r c", r=8, c=8),
                                          AX.XY, ALU.add)
                    for i in range(4):
                        ins = dve.bn_stats(bnst[:, k * 4 + i, :], xa[k % 4][:, i * 512:(i + 1) * 512])
                    ins.then_inc(s_aused, 1)
                dve.wait_ge(s_aused, im * NP + (NP + 4))
                dve.sem_inc(s_bst, 1)
                dve.bn_aggr(mvt[:, :], bnst[:, :, :]).then_inc(s_bst, 1)
                dve.wait_ge(s_bst, im * 2 + 2)
                dve.tensor_copy(mv[:, bass.ds(im, 1), :].rearrange("p a k -> p (a k)"), mvt[:, :]).then_inc(s_mv, 1)
            dve.wait_ge(s_mv, NI)

            def gn_dve(n_gp, n_pg, n_ga):
                link(dve.tensor_copy(st[:, 0, :], mv[:, :, 0]))
                dve.sem_inc(s_gp, 1)
                dve.wait_ge(s_pg, n_pg)
                link(dve.tensor_copy(st[:, 1, :], PS[:, 0, 0:NI]))
                link(dve.tensor_tensor(st[:, 2, :], st[:, 0, :], st[:, 1, :], ALU.subtract))
                link(dve.tensor_tensor(st[:, 2, :], st[:, 2, :], st[:, 2, :], ALU.mult))
                link(dve.tensor_tensor(st[:, 3, :], st[:, 2, :], mv[:, :, 1], ALU.add))
                dve.sem_inc(s_gp, 1)
                dve.wait_ge(s_pg, n_pg + 1)
                link(dve.tensor_scalar(st[:, 4, :], PS[:, 1, 0:NI], EPS, None, ALU.add))
                dve.sem_inc(s_ga, 1)
                dve.wait_ge(s_ag, n_ga)
                link(dve.reciprocal(coef[:, 0, :], st[:, 5, :]))
                link(dve.scalar_tensor_tensor(out=coef[:, 1, :], in0=st[:, 1, :], scalar=-1.0, in1=coef[:, 0, :],
                                              op0=ALU.mult, op1=ALU.mult))

            link(dve.memset(st[:, 6, :], 0.0))
            gn_dve(1, 1, 1)
            link(dve.tensor_scalar(st[:, 7, :], coef[:, 0, :], 1 / 64, None, ALU.mult))
            for i in range(NI):
                link(dve.tensor_scalar(pooled[:, i, :], pooled[:, i, :], st[:, 7, i:i + 1], coef[:, 1, i:i + 1],
                                       ALU.mult, ALU.add))
            dve.sem_inc(s_gp, 1)
            dve.wait_ge(s_pg, 3)
            link(dve.tensor_copy(sg[:, :, :], PS[:, 2, 0:NI * KK].rearrange("p (g o) -> p g o", o=KK)))
            dve.sem_inc(s_gp, 1)
            dve.wait_ge(s_pg, 4)
            link(dve.tensor_reduce(s9[:, 0, :], PS[:, 3, 0:NI * KK].rearrange("p (g o) -> p o g", o=KK), AX.X, ALU.add))
            link(dve.tensor_scalar(s9[:, 0, :], s9[:, 0, :], 1 / (NI * P), None, ALU.mult))
            for i in range(NI):
                link(dve.tensor_tensor(sgd[:, i, :], sg[:, i, :], s9[:, 0, :], ALU.subtract))
            link(dve.tensor_tensor(sq9[:, :, :], sgd[:, :, :], sgd[:, :, :], ALU.mult))
            dve.sem_inc(s_gp, 1)
            dve.wait_ge(s_pg, 5)
            link(dve.tensor_reduce(s9[:, 1, :], PS[:, 0, 0:NI * KK].rearrange("p (g o) -> p o g", o=KK), AX.X, ALU.add))
            link(dve.tensor_scalar(s9[:, 1, :], s9[:, 1, :], 1 / (NI * P), EPS, ALU.mult, ALU.add))
            dve.sem_inc(s_ga, 1)
            dve.wait_ge(s_ag, 2)
            link(dve.reciprocal(s9[:, 3, :], s9[:, 2, :]))
            dve.wait_ge(s_w, 16 * (NW + 14))
            link(dve.tensor_tensor(s9[:, 3, :], s9[:, 3, :], gam[:, :], ALU.mult))
            for i in range(NI):
                v = w9[:, i * KK:(i + 1) * KK]
                link(dve.tensor_tensor(v, sgd[:, i, :], s9[:, 3, :], ALU.mult))
                link(dve.tensor_tensor(v, v, bet[:, :], ALU.add))
            for k in range(KC):
                link(dve.tensor_tensor(wconv[:, k, :], win[:, 0:DI], cvr[:, k, :], ALU.mult))
            dve.wait_ge(s_pp, 1)
            link(dve.tensor_copy(wdx[:, :], PS[:, 4, 0:P]))
            link(dve.tensor_tensor(c_bf, PS[:, 5, 0:2], c_bfc1, ALU.add))
            link(dve.tensor_reduce(wsum[:, :], wop[:, :], AX.X, ALU.add))
            link(dve.tensor_scalar(wsum[:, :], wsum[:, :], 1 / DM, None, ALU.mult))
            link(dve.tensor_scalar(wop[:, :], wop[:, :], wsum[:, 0:1], None, ALU.subtract))
            link(dve.tensor_scalar(wfc1[:, :], wfc1r[:, :], c_g1, None, ALU.mult))
            dve.wait_ge(s_an, 1)
            link(dve.tensor_scalar(aneg[:, :], aneg[:, :], -1.0, None, ALU.mult))
            link(dve.tensor_scalar(c_scale, c_bnv, EPS, None, ALU.add))
            dve.sem_inc(s_ga, 1)
            dve.wait_ge(s_ag, 3)
            link(dve.reciprocal(c_tmp, c_tmp))
            link(dve.tensor_tensor(c_scale, c_tmp, c_bng, ALU.mult))
            link(dve.tensor_tensor(c_tmp, c_scale, c_bnm, ALU.mult))
            link(dve.tensor_tensor(c_shift, c_bnb, c_tmp, ALU.subtract))
            dve.sem_inc(s_prep, 1)
            dve.wait_ge(s_cst, 4)
            for i in range(2):
                for col in (0, 129):
                    link(dve.memset(xh[i][:, :, col:col + 1], 0.0))
            dve.sem_inc(s_ga, 1)
            dve.sem_inc(s_bused, 2)
            dve.sem_inc(s_htap, 2)
            dve.sem_inc(s_tapr, 2)
            dve.sem_inc(s_x1free, 2)
            base = steps[0]
            per = NJ * (NP * (1 + len(DVE_TAPS)) + 2)
            with dve.Fori(0, NB) as b:
                done = [0]

                def link_b(ins):
                    done[0] += 1
                    ins.then_inc(s_dv, 1)
                    dve.wait_ge(s_dv, b * per + (base + done[0]))
                for j in range(NJ):
                    w0 = (b * NJ + j) * KK
                    dve.wait_ge(s_taps, b * (NJ * NP) + (j * NP - NP + 2) if j else b * (NJ * NP) + 2)
                    for i, tap in enumerate(PE_TAPS):
                        ins = dve.tensor_scalar(dgw[:, j, i, :], ident[:, :], w9[:, bass.ds(w0 + tap, 1)], None, ALU.mult)
                    ins.then_inc(s_diag, 1)
                    for k in range(NP):
                        n = b * (NJ * NP) + (j * NP + k)
                        acc = x1t[k % 2].rearrange("p (r c) -> p r c", c=WW)
                        dve.wait_ge(s_taps, n + 3)
                        dve.wait_ge(s_x1free, n + 1)
                        link_b(dve.tensor_tensor(acc, xb[k % 2][:, 1:17, :],
                                                 PS[:, 4 * (k % 2):4 * (k % 2) + 4, :].rearrange(
                                                     "p a (r c) -> p (a r) c", c=WW), ALU.add))
                        dve.sem_inc(s_bused, 1)
                        dve.sem_inc(s_tapr, 1)
                        for tap in DVE_TAPS:
                            dy, dx = tap // 3, tap % 3
                            link_b(dve.scalar_tensor_tensor(out=acc, in0=xh[k % 2][:, dy:dy + PR, dx:dx + WW],
                                                            scalar=w9[:, bass.ds(w0 + tap, 1)], in1=acc,
                                                            op0=ALU.mult, op1=ALU.add))
                        dve.sem_inc(s_htap, 1)
                        dve.sem_inc(s_x1, 1)
                        for i in range(4):
                            ins = dve.bn_stats(bnst[:, k * 4 + i, :], x1t[k % 2][:, i * 512:(i + 1) * 512])
                    link_b(ins)
                    dve.sem_inc(s_bst, 1)
                    link_b(dve.bn_aggr(mvt[:, :], bnst[:, :, :]))
                    dve.tensor_copy(mv[:, bass.ds(b * NJ + j, 1), :].rearrange("p a k -> p (a k)"), mvt[:, :]).then_inc(s_mv, 1)
            dve.wait_ge(s_mv, 2 * NI)
            steps[0] = base + NB * per
            gn_dve(6, 6, 4)
            for b in range(NB):
                for i in range(2):
                    link(dve.tensor_copy(coefU[:, b * UPB:(b + 1) * UPB, 2 * i:2 * i + 2],
                                         coef[:, i:i + 1, b * NJ:(b + 1) * NJ].to_broadcast([P, UPB, NJ])))
            dve.sem_inc(s_coef, 1)
            dve.wait_ge(s_c, 1)
            dve.sem_inc(u_res, 1)
            dve.sem_inc(u_free, 1)

            def norm_hat(u):
                dve.wait_ge(u_xl, (u + 1) * 16)
                for j in range(NJ):
                    ins = dve.tensor_scalar(xhat[:, j, :], xl[:, j * T:(j + 1) * T], coefU[:, bass.ds(u, 1), j:j + 1].rearrange("p a k -> p (a k)"),
                                            coefU[:, bass.ds(u, 1), 2 + j:3 + j].rearrange("p a k -> p (a k)"), ALU.mult, ALU.add)
                ins.then_inc(u_hat, 1)

            def norm_centre(u):
                dve.wait_ge(u_mean, u + 1)
                for j in range(NJ):
                    ins = dve.tensor_tensor(xhat[:, j, :], xhat[:, j, :], PS[:, 7, :], ALU.subtract)
                ins.then_inc(u_cen, 1)

            def norm_out(u, start):
                if not start:
                    dve.tensor_scalar(xn[:, :, 0:3], xn[:, :, T:T + 3], keep[:, bass.ds(u - 1, 1)], None,
                                      ALU.mult).then_inc(u_hist, 1)
                    dve.wait_ge(u_hist, u)
                dve.wait_ge(u_rstd, u + 1)
                for j in range(NJ):
                    ins = dve.scalar_tensor_tensor(out=xhat[:, j, :], in0=xhat[:, j, :], scalar=c_gn[:, j:j + 1],
                                                   in1=rstd[:, :], op0=ALU.mult, op1=ALU.mult)
                ins.then_inc(u_xg, 1)
                dve.wait_ge(u_xg, u + 1)
                for j in range(NJ):
                    ins = dve.tensor_scalar(xn[:, j, 3:], xhat[:, j, :], c_bn[:, j:j + 1], None, ALU.add)
                ins.then_inc(u_xn, 1)

            W01 = PS[:, 5:7, :].rearrange("p a t -> p (a t)")

            def z_copy(u, j):
                dve.wait_ge(p_z, 2 * u + j + 1)
                dve.tensor_copy(sz[:, j, :], W01).then_inc(p_zc, 1)

            def dt_read(u, j):
                s = 2 * u + j
                dve.wait_ge(p_dt, s + 1)
                dve.tensor_scalar(rlu[:, :], W01, c_bdt, 0.0, ALU.add, ALU.max).then_inc(p_rl, 1)
                dve.wait_ge(p_rl, s + 1)
                dve.scalar_tensor_tensor(out=vab[:, :], in0=rlu[:, :], scalar=-2.0, in1=W01,
                                         op0=ALU.mult, op1=ALU.add).then_inc(p_dtv, 1)

            def dt_sum(u, j):
                s = 2 * u + j
                dve.wait_ge(p_ln, s + 1)
                dve.tensor_tensor(dt[:, j, :], vab[:, :], rlu[:, :], ALU.add).then_inc(p_dts, 1)
                dve.wait_ge(p_dts, s + 1)
                dve.tensor_tensor(du[:, j, :], dt[:, j, :], xc[:, j, :], ALU.mult).then_inc(p_u, 1)

            def bc_rest(u, j):
                dve.wait_ge(p_h, 2 * u + j + 1)
                dve.tensor_tensor(res3[:, :], PS[0:64, 5:7, :].rearrange("p a t -> p (a t)"), spl[0:64, j, :],
                                  ALU.subtract).then_inc(p_r, 1)

            def bc_low(u, j):
                dve.wait_ge(p_m, 2 * u + j + 1)
                dve.tensor_tensor(spl[0:32, j, :], res3[0:32, :], spl[0:32, j, :], ALU.subtract).then_inc(p_l, 1)

            def y_copy(u, j):
                dve.wait_ge(p_op, 2 * u + j + 1)
                dve.tensor_copy(ymc[:, :], PS[:, 7, :]).then_inc(p_ymc, 1)

            def y_norm(u, j):
                dve.wait_ge(p_yrs, 2 * u + j + 1)
                dve.tensor_tensor(yn[:, :], ymc[:, :], yrs[:, :], ALU.mult).then_inc(p_yn, 1)

            def fc1_copy(u, j):
                dve.wait_ge(p_f1a, 2 * u + j + 1)
                dve.tensor_copy(gel, W01).then_inc(p_f1c, 1)

            def mix_in(u, j):
                s = 2 * u + j
                dve.wait_ge(p_f2, s + 1)
                dve.wait_ge(p_xk, s + 1)
                dve.tensor_tensor(xi[:, j, :], PS[:, 7, :], xk[:, j, :], ALU.add).then_inc(p_xi, 1)

            def result(u):
                dve.wait_ge(u_fin, u + 1)
                dve.wait_ge(u_xr, (u + 1) * 16)
                dve.wait_ge(u_free, u + 1)
                dve.tensor_tensor(ob, xres, sq[:, :, :].rearrange("p j t -> p (j t)"), ALU.add).then_inc(u_res, 1)

            def drive_q(u, j, q):
                g = u * (2 * NQ) + (j * NQ + q)
                c = q // NS
                dve.wait_ge(q_b, g + 1)
                dve.tensor_tensor(drive[:, q % RING, :], du[:, j, c * T:(c + 1) * T], PS[:, q % 2, :],
                                  ALU.mult).then_inc(q_drv, 1)

            def scan_q(u, j, q, first):
                g = u * (2 * NQ) + (j * NQ + q)
                dve.wait_ge(q_drv, g + 1)
                dve.wait_ge(q_exp, g + 1)
                if not (first and j == 0 and q < RING):
                    dve.wait_ge(q_prod, g - (RING - 1))
                k = j * NQ + q
                dve.tensor_tensor_scan(hst[:, q % RING, :], decay[:, q % RING, :], drive[:, q % RING, :],
                                       init[:, k:k + 1], ALU.mult, ALU.add).then_inc(q_scan, 1)

            def y_end(u, j, c):
                s = 2 * u + j
                dve.wait_ge(q_sum, s * NQ + (c + 1) * NS)
                wait(dve, k_yz, 0)
                dve.scalar_tensor_tensor(out=ytmp[:, :], in0=xc[:, j, c * T:(c + 1) * T], scalar=c_D,
                                         in1=PS[:, 4, :], op0=ALU.mult, op1=ALU.add).then_inc(k_y, 1)
                dve.wait_ge(k_y, s * 2 + (c + 1))
                wait(dve, p_op, s)
                dve.tensor_tensor(yz[:, c, :], ytmp[:, :], sz[:, j, c * T:(c + 1) * T], ALU.mult).then_inc(k_yz, 1)

            def unit(u, first, last):
                for j in range(2):
                    for q in range(NQ):
                        if q + 1 < NQ:
                            drive_q(u, j, q + 1)
                        elif j == 0:
                            drive_q(u, 1, 0)
                        elif not last:
                            drive_q(u + 1, 0, 0)
                        scan_q(u, j, q, first)
                        nu, nj = (u, 1) if j == 0 else (u + 1, 0)
                        bu, bj = (u - 1, 1) if j == 0 else (u, 0)
                        front = not (last and j == 1)
                        back = not (first and j == 0)
                        if q == S_YEND and back:
                            y_end(bu, bj, 1)
                        if q == NS + S_YEND:
                            y_end(u, j, 0)
                        if j == 1 and not last:
                            if q == S_HAT:
                                norm_hat(nu)
                            if q == S_CEN:
                                norm_centre(nu)
                            if q == S_XN:
                                norm_out(nu, False)
                        if front:
                            if q == S_ZC:
                                z_copy(nu, nj)
                            if q == S_DTV:
                                dt_read(nu, nj)
                            if q == S_DTU:
                                dt_sum(nu, nj)
                            if q == S_BCR:
                                bc_rest(nu, nj)
                            if q == S_BCL:
                                bc_low(nu, nj)
                        if back:
                            if q == S_YMC:
                                y_copy(bu, bj)
                            if q == S_YN:
                                y_norm(bu, bj)
                            if q == S_FC1C:
                                fc1_copy(bu, bj)
                            if q == S_XI:
                                mix_in(bu, bj)
                            if q == S_RES and j == 0:
                                result(bu)

            norm_hat(0)
            norm_centre(0)
            norm_out(0, True)
            z_copy(0, 0)
            dt_read(0, 0)
            dt_sum(0, 0)
            bc_rest(0, 0)
            bc_low(0, 0)
            drive_q(0, 0, 0)
            unit(0, True, False)
            with dve.Fori(1, NU - 1) as u:
                unit(u, False, False)
            unit(NU - 1, False, True)
            y_end(NU - 1, 1, 1)
            y_copy(NU - 1, 1)
            y_norm(NU - 1, 1)
            fc1_copy(NU - 1, 1)
            mix_in(NU - 1, 1)
            result(NU - 1)


def kernel(**inputs):
    import numpy as _np
    import concourse.bacc as _bacc
    from concourse import mybir as _mybir
    from concourse.bass_utils import run_bass_kernel_spmd as _run

    nc = _bacc.Bacc("TRN2", target_bir_lowering=False, num_devices=1)
    i = {k.replace("L0_conv_", "L0").replace("L1_conv_", ""): _np.asarray(v) for k, v in inputs.items()}
    arranged = [
        ("x", i["x"]), ("w_conv", i["L0w_conv"].T), ("gamma", i["L0gamma"]), ("beta", i["L0beta"]),
        ("g_norm", i["g_norm"]), ("b_norm", i["b_norm"]), ("g_norm1", i["g_norm1"]), ("b_norm1", i["b_norm1"]),
        ("W_inT", i["W_in"].T), ("W_cv", i["W_conv"].reshape(DI, KC).T.reshape(-1)), ("b_conv", i["b_conv"]),
        ("W_xp", i["W_xproj"]), ("W_xpT", i["W_xproj"].T), ("W_dtT", i["W_dt"].T), ("b_dt", i["b_dt"]),
        ("A_log", i["A_log"]), ("D_par", i["D_par"]), ("W_outpT", i["W_outp"].T), ("skip", i["skip_scale"]),
        ("W_fc1T", i["W_fc1"].T), ("b_fc1", i["b_fc1"]), ("W_fc2T", i["W_fc2"].T), ("b_fc2", i["b_fc2"]),
        ("W_outT", i["W_out"].T.reshape(DM, 4, CH).transpose(1, 0, 2).reshape(CH, CH)), ("bn_g", i["bn_g"]), ("bn_b", i["bn_b"]), ("bn_m", i["bn_mean"]),
        ("bn_v", i["bn_var"]),
    ]
    arrays, args = {}, []
    for name, a in arranged:
        a = _np.ascontiguousarray(a)
        arrays[f"in_{name}"] = a
        args.append(nc.dram_tensor(f"in_{name}", a.shape, _mybir.dt.from_np(a.dtype), kind="ExternalInput").ap())
    args.append(nc.dram_tensor("out_y", (NB, CH, HH, WW), _mybir.dt.float32, kind="ExternalOutput").ap())
    build(nc, *args)
    r = _run(nc, [arrays], core_ids=[0])
    return r.results[0]["out_y"]
```

```python
from contextlib import ExitStack

import concourse.bass as bass
from concourse import mybir

F32 = mybir.dt.float32
BF16 = mybir.dt.bfloat16
ALU = mybir.AluOpType
ACT = mybir.ActivationFunctionType
AX = mybir.AxisListType

NB, CH, HH, WW = 4, 256, 128, 128
HW = HH * WW
P = 128
NJ = CH // P
NI = NB * NJ
KK = 9
EPS = 1e-5
DM, DI, NS, KC, RK = 64, 128, 16, 4, 4
T = 512
NU = NB * HW // T
UPB = HW // T
NQ = 2 * NS
PX = 2048
NP = HW // PX
PR = PX // WW
PE_TAPS = (0, 1, 2, 3)
DVE_TAPS = (4, 5, 6, 7, 8)
RING = 4
EXP_LN = "natural_log_exp_and_others"

LEAD_B, LEAD_C, LEAD_EXP, LEAD_CC, LEAD_DRV, LAG = 2, -1, 4, -1, 1, 6
DEEP = 8
ADDED = (2, 6, 10, 14)

F_Z, F_ZC, F_CONV, F_SILU, F_DT, F_DTV, F_E, F_BC = 10, 11, 12, 16, 20, 21, 22, 22
F_W, F_LN, F_REST, F_HI, F_RES, F_MID, F_LO, F_DTU = 23, 24, 22, 23, 24, 25, 26, 26
B_OUTP, B_YMC, B_YSQ, B_YVAR, B_YRSTD, B_YN = 10, 11, 12, 13, 14, 15
B_FC1, B_FC1C, B_GELU, B_FC2, B_XI, B_XK = 25, 26, 28, 32, 33, 34
U_LOADX, U_WOUT, U_FIN, U_RES = 3, 34, 38, 40
U_HAT, U_MEAN, U_CEN, U_SQ, U_VAR, U_RSTD, U_XN, U_SHIFT = 35, 36, 37, 38, 39, 40, 41, 42


def split_slot(slot):
    return slot // (2 * NQ), slot % (2 * NQ)


def build(nc, x, w_conv, gamma, beta, g_norm, b_norm, g_norm1, b_norm1, W_inT, W_cv, b_conv, W_xp, W_xpT, W_dtT,
          b_dt, A_log, D_par, W_outpT, skip, W_fc1T, b_fc1, W_fc2T, b_fc2, W_outT, bn_g, bn_b, bn_m, bn_v, out):
    with ExitStack() as ctx:
        def sb(name, shape, dt=F32):
            return ctx.enter_context(nc.sbuf_tensor(name, shape, dt))

        def sem(name):
            return ctx.enter_context(nc.semaphore(name))

        PS = ctx.enter_context(nc.psum_tensor("PS", [P, 8, 512], F32))
        x1s = nc.dram_tensor("x1_scratch", (NU, P, NJ, T), F32, kind="Internal").ap()

        AW = 4096 + 3 * 8 * T + 6 * T
        XR0, XR1 = 18 * WW, 18 * 130
        arena = sb("arena", [P, AW])
        xa = [arena[:, i * PX:(i + 1) * PX] for i in range(4)]
        xb = [arena[:, i * XR0:(i + 1) * XR0].rearrange("p (r c) -> p r c", c=WW) for i in range(2)]
        o = 2 * XR0
        xh = [arena[:, o + i * XR1:o + (i + 1) * XR1].rearrange("p (r c) -> p r c", c=130) for i in range(2)]
        o += 2 * XR1
        x1t = [arena[:, o + i * PX:o + (i + 1) * PX] for i in range(2)]
        assert o + 2 * PX <= AW

        def ring(k):
            return arena[:, k * RING * T:(k + 1) * RING * T].rearrange("p (r t) -> p r t", t=T)
        drive, csb = [ring(k) for k in range(2)]
        o = 2 * RING * T
        decay, hst, prod = [arena[:, o + k * DEEP * T:o + (k + 1) * DEEP * T].rearrange("p (r t) -> p r t", t=T)
                            for k in range(3)]
        o += 3 * DEEP * T
        xres = arena[:, o:o + 2 * T]
        gel = [arena[:, o + 2 * T:o + 4 * T], arena[:, o + 4 * T:o + 6 * T]]
        assert o + 6 * T <= AW

        ident = sb("ident", [P, P])
        grp8 = sb("grp8", [P, P])
        ones = sb("ones", [P, P])
        mean256 = sb("mean256", [P, P])
        half64 = sb("half64", [P, P])
        sel = sb("sel", [3 * 2 * NS, 2 * NS, P], BF16)
        zrow = sb("zrow", [P, 130])
        wcT = sb("wcT", [P, NJ, KK])
        gam = sb("gam", [P, KK])
        bet = sb("bet", [P, KK])
        cvr = sb("cvr", [P, KC, P])
        wconv = sb("wconv", [P, 2, KC // 2, P])
        win = sb("win", [P, 2 * DI])
        wxp = sb("wxp", [RK, P])
        wdt = sb("wdt", [RK, P])
        wdx = sb("wdx", [P, P])
        wbc = sb("wbc", [P, 3 * 2 * NS])
        wop = sb("wop", [P, DM])
        wsum = sb("wsum", [P, 1])
        wfc1r = sb("wfc1r", [P, 4 * DM])
        wfc1 = sb("wfc1", [P, 4 * DM])
        wfc2 = sb("wfc2", [P, 2, DM])
        wout = sb("wout", [P, NJ, CH])
        cols = sb("cols", [P, 40])
        (c_bconv, c_bdt, c_D, c_skip, c_b2, c_g1, c_b1, c_eps, c_one) = [cols[:, i:i + 1] for i in range(9)]
        c_bfc1, c_gn, c_bn, c_bng, c_bnb, c_bnm, c_bnv = [cols[:, 10 + 2 * i:12 + 2 * i] for i in range(7)]
        c_scale, c_shift, c_tmp = [cols[:, 24 + 2 * i:26 + 2 * i] for i in range(3)]
        c_bf = cols[:, 30:32]
        aneg = sb("aneg", [P, NS])
        keep = sb("keep", [P, NU])
        keepc = sb("keepc", [P, 1])
        pooled = arena[:, 4 * PX:4 * PX + NI * 256].rearrange("p (i w) -> p i w", i=NI)
        bnst = sb("bnst", [P, 32, 6])
        mvt = sb("mvt", [P, 2])
        mv = sb("mv", [P, NI, 2])
        st = sb("st", [P, 8, NI])
        coef = sb("coef", [P, 2, NI])
        coefU = sb("coefU", [P, NU, 4])
        sg = sb("sg", [P, NI, KK])
        sgd = sb("sgd", [P, NI, KK])
        sq9 = sb("sq9", [P, NI, KK])
        s9 = sb("s9", [P, 4, KK])
        w9 = sb("w9", [P, NI * KK])
        dgw = sb("dgw", [P, 2, len(PE_TAPS), P])

        init = sb("init", [P, 4 * NS])
        xl = sb("xl", [P, 2 * T])
        xhat = sb("xhat", [P, NJ, T])
        fin = sb("fin", [P, NJ, T])
        rstd = sb("rstd", [P, T])
        xn = sb("xn", [P, NJ, 2, 3 + T])
        c_kb = sb("c_kb", [P, NJ])
        xk = sb("xk", [P, NJ, T])
        xi = sb("xi", [P, NJ, T])
        xc = sb("xc", [P, 2, 2 * T])
        sz = sb("sz", [P, 2, 2 * T])
        dt = sb("dt", [P, 2, 2 * T])
        du = sb("du", [P, 2, 2 * T])
        rlu = sb("rlu", [P, 2 * T])
        vab = sb("vab", [P, 2 * T])
        res3 = sb("res3", [DM, 2 * T])
        spl = sb("spl", [3 * 2 * NS, 2, 2 * T], BF16)
        ytmp = sb("ytmp", [P, T])
        yz = sb("yz", [P, 2, T])
        ymc = sb("ymc", [P, T])
        ysq = sb("ysq", [P, T])
        yrs = ysq
        yn = sb("yn", [P, T])
        wlog = sb("wlog", [P, 2 * T])
        sq = wlog[:, :].rearrange("p (j t) -> p j t", j=NJ)
        wrest = sb("wrest", [P, 2 * T])

        s_w = sem("weights_loaded")
        s_cst = sem("constants_made")
        s_za = sem("fill_done")
        s_aload = [sem(f"a_loaded{i}") for i in range(4)]
        s_aused = sem("a_used")
        s_dv = sem("dve_step")
        s_gp = sem("gn_to_pe")
        s_pg = sem("pe_to_gn")
        s_ga = sem("gn_to_act")
        s_ag = sem("act_to_gn")
        s_prep = sem("weights_ready")
        s_an = sem("a_negated")
        s_pp = sem("prep_from_pe")
        s_bload = [sem(f"b_loaded{i}") for i in range(2)]
        s_bused = sem("b_used")
        s_hat = sem("padded_ready")
        s_htap = sem("padded_used_dve")
        s_taps = sem("pe_taps_done")
        s_tapr = sem("pe_taps_read")
        s_diag = sem("diag_ready")
        s_x1 = sem("x1_ready")
        s_st = sem("x1_stored")
        s_x1free = sem("x1_buffer_free")
        u_free = sem("u_result_buffer_free")
        s_bst = sem("b_step")
        s_coef = sem("coefs_ready")
        s_c = sem("stage_c_start")
        s_mv = sem("statistics_kept")
        s_keep = sem("keep_copied")
        q_b, q_c, q_exp, q_cc = sem("q_B_ready"), sem("q_C_ready"), sem("q_decay_ready"), sem("q_C_copied")
        q_drv, q_scan, q_prod, q_sum = sem("q_drive_ready"), sem("q_scanned"), sem("q_product_ready"), sem("q_summed")
        k_y, k_yz = sem("k_y_read"), sem("k_yz_ready")
        u_xl, u_hat, u_mean, u_cen = sem("u_x_loaded"), sem("u_hat"), sem("u_mean"), sem("u_centred")
        u_sq, u_var, u_rstd, u_xg, u_xn = sem("u_sq"), sem("u_var"), sem("u_rstd"), sem("u_xg"), sem("u_xn")
        u_ln, u_hist = sem("u_lnvar"), sem("u_hist")
        q_add, u_shift, p_w, p_rest, p_dtin = (sem("q_added"), [sem(f"u_shifted{j}") for j in range(NJ)], sem("p_1_plus_e"), sem("p_log_rest"),
                                               sem("p_dt_first_part"))
        u_wout, u_fin, u_res, u_xr, u_out = (sem("u_wout"), sem("u_fin"), sem("u_res"), sem("u_xres_loaded"),
                                             sem("u_stored"))
        p_z, p_zc, p_conv, p_silu = sem("p_z"), sem("p_z_copied"), sem("p_conv"), sem("p_silu")
        p_rl = sem("p_dt_positive")
        p_dt, p_dtv, p_ln, p_e, p_dts, p_u = (sem("p_dt"), sem("p_dt_read"), sem("p_ln"), sem("p_e"), sem("p_dt_sum"),
                                              sem("p_u"))
        p_bc, p_h, p_r, p_m, p_l = sem("p_bc"), sem("p_hi"), sem("p_rest"), sem("p_mid"), sem("p_lo")
        p_op, p_ymc, p_ysq, p_yvar, p_yln, p_yrs, p_yn = [sem(f"p_{n}") for n in
                                                         ("outp", "ymc", "ysq", "yvar", "yln", "yrs", "yn")]
        p_f1, p_f1c, p_gel, p_f2, p_xi, p_xk = [sem(f"p_{n}") for n in
                                                       ("fc1", "fc1_copied", "gelu", "fc2", "xi", "xk")]

        xv = x.rearrange("b c h w -> (b c) (h w)")
        xrow = x.rearrange("b c h w -> (b c) h w")
        outv = out.rearrange("b (j p) h w -> b p j (h w)", p=P)
        NW = 27

        block = ctx.enter_context(nc.Block())

        def wait(eng, s, v):
            if isinstance(v, int) and v <= 0:
                return
            eng.wait_ge(s, v)

        def exists(u):
            return not isinstance(u, int) or 0 <= u < NU

        def run(u, slot, step, at, j, c=None):
            home = j * NQ + (at - NQ if step in front_steps else at + NQ)
            du, s = split_slot(home)
            if s == slot and exists(u - du):
                step(u - du, j) if c is None else step(u - du, j, c)
        front_steps = []

        @block.sync
        def _(sp):
            loads = [
                (wcT[:, :, :], w_conv.rearrange("(j p) o -> p j o", p=P)),
                (gam[:, :], gamma.rearrange("(a k) -> a k", a=1).to_broadcast([P, KK])),
                (bet[:, :], beta.rearrange("(a k) -> a k", a=1).to_broadcast([P, KK])),
                (win[0:DM, :], W_inT), (win[DM:P, :], W_inT),
                (cvr[:, :, :].rearrange("p k d -> p (k d)"), W_cv.rearrange("(a k) -> a k", a=1).to_broadcast([P, KC * DI])),
                (wxp[:, :], W_xp[0:RK, :]), (wdt[:, :], W_dtT),
                (wbc[:, 0:32], W_xpT[:, RK:]), (wbc[:, 32:64], W_xpT[:, RK:]), (wbc[:, 64:96], W_xpT[:, RK:]),
                (wop[:, :], W_outpT), (wfc1r[0:DM, :], W_fc1T), (wfc1r[DM:P, :], W_fc1T),
                (wfc2[:, :, :], W_fc2T.rearrange("(h p) m -> p h m", p=P)),
                (wout[:, :, :], W_outT.rearrange("(j p) o -> p j o", p=P)),
                (aneg[:, :], A_log),
                (c_skip, skip.rearrange("(a k) -> a k", a=1).to_broadcast([P, 1])),
            ]
            for col, v in ((c_bconv, b_conv), (c_bdt, b_dt), (c_D, D_par)):
                loads.append((col, v.rearrange("(p a) -> p a", a=1)))
            for col, v in ((c_b2, b_fc2), (c_g1, g_norm1), (c_b1, b_norm1)):
                for h in range(2):
                    loads.append((col[DM * h:DM * h + DM, :], v.rearrange("(p a) -> p a", a=1)))
            assert len(loads) == NW
            for col, v in ((c_bfc1, b_fc1), (c_gn, g_norm), (c_bn, b_norm), (c_bng, bn_g), (c_bnb, bn_b),
                           (c_bnm, bn_m), (c_bnv, bn_v)):
                for j in range(2):
                    loads.append((col[:, j:j + 1], v[P * j:P * j + P].rearrange("(p a) -> p a", a=1)))
            for dst, src in loads:
                sp.dma_start(dst, src).then_inc(s_w, 16)
            with sp.Fori(0, NI) as im:
                for k in range(NP):
                    sp.wait_ge(s_aused, im * NP + (k + 1))
                    sp.dma_start(xa[k % 4], xv[bass.ds(im * P, P), k * PX:(k + 1) * PX]).then_inc(s_aload[k % 4], 16)
            sp.wait_ge(s_aused, NI * NP + 4)
            with sp.Fori(0, NB) as b:
                for j in range(NJ):
                    for k in range(NP):
                        lo, hi = (1 if k == 0 else 0), (17 if k == NP - 1 else 18)
                        r0 = k * PR - 1 + lo
                        sp.wait_ge(s_bused, b * (NJ * NP) + (j * NP + k + 1))
                        sp.dma_start(xb[k % 2][:, lo:hi, :],
                                     xrow[bass.ds(b * CH + j * P, P), r0:r0 + hi - lo, :]).then_inc(s_bload[k % 2], 16)
            sp.wait_ge(s_c, 1)
            with sp.Fori(0, NB) as b:
                with sp.Fori(0, UPB) as t:
                    u = sp.snap(b * UPB + t)
                    sp.wait_ge(u_res, u + 1)
                    sp.dma_start(xres.rearrange("p (a j t) -> p a j t", a=1, j=NJ),
                                 x1s[bass.ds(u, 1)].rearrange("u p j t -> p u j t")).then_inc(u_xr, 16)
                    sp.wait_ge(u_res, u + 2)
                    sp.dma_start(outv[bass.ds(b, 1), :, :, bass.ds(t * T, T)].rearrange("b p j t -> p b j t"),
                                 fin[:, :, :].rearrange("p (a j) t -> p a j t", a=1)).then_inc(u_out, 16)
                    sp.wait_ge(u_out, 16 * (u + 1))
                    sp.sem_inc(u_free, 1)

        @block.gpsimd
        def _(pool):
            fills = [(ident, 0.0), (grp8, 1 / 8), (ones, 1.0), (mean256, 1 / CH), (half64, 1 / DM), (sel, 0.0),
                     (zrow, 0.0), (keep, 1.0)]
            for tile, v in fills:
                pool.memset(tile[:], v).then_inc(s_za, 1)
            pool.wait_ge(s_za, len(fills))
            pool.affine_select(out=ident[:, :], in_=ident[:, :], compare_op=ALU.not_equal, fill=1.0, base=0,
                               pattern=[[-1, P]], channel_multiplier=1).then_inc(s_cst, 1)
            k = len(fills)
            for tile, g in ((grp8, 8), (half64, DM)):
                v = tile[:, :].rearrange("p (g e) -> p g e", e=g)
                pool.affine_select(out=v, in_=v, compare_op=ALU.is_ge, fill=0.0, base=0,
                                   pattern=[[-g, P // g], [0, g]], channel_multiplier=1).then_inc(s_za, 1)
                k += 1
                pool.wait_ge(s_za, k)
                pool.affine_select(out=v, in_=v, compare_op=ALU.is_ge, fill=0.0, base=g - 1,
                                   pattern=[[g, P // g], [0, g]], channel_multiplier=-1).then_inc(s_cst, 1)
            for r in range(3):
                pool.affine_select(out=sel[:, :, :], in_=sel[:, :, :], compare_op=ALU.not_equal, fill=1.0,
                                   base=-32 * r, pattern=[[-1, 2 * NS], [0, P]], channel_multiplier=1).then_inc(s_za, 1)
                k += 1
                pool.wait_ge(s_za, k)
            pool.memset(keep[:, UPB - 1:NU:UPB], 0.0).then_inc(s_cst, 1)
            with pool.Fori(0, NB) as b:
                for j in range(NJ):
                    for k in range(NP):
                        pool.wait_ge(s_x1, b * (NJ * NP) + (j * NP + k + 1))
                        pool.dma_start(x1s[bass.ds(b * UPB + k * (PX // T), PX // T), :, j, :].rearrange("u p t -> p u t"),
                                       x1t[k % 2].rearrange("p (u t) -> p u t", t=T)).then_inc(s_st, 16)
                        pool.wait_ge(s_st, b * (16 * NJ * NP) + 16 * (j * NP + k + 1))
                        pool.sem_inc(s_x1free, 1)
            pool.wait_ge(s_coef, 1)
            pool.sem_inc(s_c, 1)

            def keep_flag(u):
                wait(pool, q_prod, u * (2 * NQ))
                pool.sem_inc(s_keep, 1)
                pool.tensor_copy(keepc[:, :], keep[:, bass.ds(u, 1)]).then_inc(s_keep, 1)
                pool.wait_ge(s_keep, 2 * u + 2)

            def product(u, q):
                g = u * (2 * NQ) + q
                n, r = q % NS, q % DEEP
                pool.wait_ge(q_scan, g + 1)
                pool.tensor_tensor(init[:, q:q + 1], hst[:, r, T - 1:T], keepc[:, :], ALU.mult)
                pool.wait_ge(q_cc, g + 1)
                if not (isinstance(u, int) and u == 0 and q < DEEP):
                    pool.wait_ge(q_sum, g - (DEEP - 1))
                pool.tensor_tensor(prod[:, q % DEEP, :], hst[:, r, :], csb[:, q % RING, :], ALU.mult).then_inc(q_prod, 1)
                if n in ADDED:
                    pool.wait_ge(q_prod, g + 1)
                    pool.tensor_tensor(prod[:, q % DEEP, :], prod[:, q % DEEP, :], prod[:, (q - 1) % DEEP, :],
                                       ALU.add).then_inc(q_add, 1)

            def dt_first(u, j, c):
                k = (2 * u + j) * 2 + c + 1
                pool.wait_ge(p_rest, k)
                t = slice(c * T, (c + 1) * T)
                pool.tensor_tensor(rlu[:, t], rlu[:, t], wrest[:, t], ALU.subtract).then_inc(p_dtin, 1)

            def emit(u):
                if not (isinstance(u, int) and not 0 <= u < NU):
                    keep_flag(u)
                for q in range(2 * NQ):
                    if not (isinstance(u, int) and not 0 <= u < NU):
                        product(u, q)
                    for j in range(2):
                        for c in range(2):
                            run(u, q, dt_first, F_REST + c, j, c)

            front_steps.append(dt_first)
            emit(-1)
            emit(0)
            with pool.Fori(1, NU - 1) as u:
                emit(u)
            emit(NU - 1)

        @block.scalar
        def _(act):
            act.wait_ge(s_w, 16 * (NW + 14))
            act.activation(aneg[:, :], aneg[:, :], ACT.Exp).then_inc(s_an, 1)

            def gn_sqrt(n):
                act.wait_ge(s_ga, n)
                act.activation(st[:, 5, :], st[:, 4, :], ACT.Sqrt).then_inc(s_ag, 1)
            gn_sqrt(1)
            act.wait_ge(s_ga, 2)
            act.activation(s9[:, 2, :], s9[:, 1, :], ACT.Sqrt).then_inc(s_ag, 1)
            act.wait_ge(s_ga, 3)
            act.activation(c_tmp, c_scale, ACT.Sqrt).then_inc(s_ag, 1)
            act.wait_ge(s_ga, 4)
            with act.Fori(0, NB) as b:
                for j in range(NJ):
                    for k in range(NP):
                        n = b * (NJ * NP) + (j * NP + k)
                        lo, hi = (1 if k == 0 else 0), (17 if k == NP - 1 else 18)
                        act.wait_ge(s_bload[k % 2], b * (8 * NJ * NP) + 16 * ((j * NP + k) // 2 + 1))
                        act.wait_ge(s_htap, n + 1)
                        act.wait_ge(s_taps, n + 1)
                        if k == 0:
                            act.activation(xh[0][:, 0, :], zrow[:, :], ACT.Copy)
                        if k == NP - 1:
                            act.activation(xh[1][:, 17, :], zrow[:, :], ACT.Copy)
                        act.sem_inc(s_an, 1)
                        act.activation(xh[k % 2][:, lo:hi, 1:129], xb[k % 2][:, lo:hi, :], ACT.Identity,
                                       bias=coef[:, 1, bass.ds(b * NJ + j, 1)],
                                       scale=coef[:, 0, bass.ds(b * NJ + j, 1)]).then_inc(s_hat, 1)
            gn_sqrt(5)
            act.wait_ge(s_c, 1)
            act.preload_act_table_set(EXP_LN)

            def load_x(u):
                act.dma_start(xl[:, :].rearrange("p (a j t) -> p a j t", a=1, j=NJ),
                              x1s[bass.ds(u, 1)].rearrange("u p j t -> p u j t")).then_inc(u_xl, 16)

            def shift(u, j):
                act.wait_ge(u_xn, u * NJ + (j + 1))
                for c in range(2):
                    own, other = slice(c * DM, c * DM + DM), slice((1 - c) * DM, (1 - c) * DM + DM)
                    act.dma_start(xn[other, j, c, 1:3 + T], xn[own, j, c, 0:2 + T]).then_inc(u_shift[j], 16)

            def norm_sq(u):
                act.wait_ge(u_cen, u + 1)
                act.activation(sq[:, :, :], xhat[:, :, :], ACT.Square).then_inc(u_sq, 1)

            def norm_rstd(u):
                act.wait_ge(u_var, u + 1)
                act.activation(rstd[:, :], PS[:, 7, :], ACT.Ln, bias=c_eps).then_inc(u_ln, 1)
                act.wait_ge(u_ln, u + 1)
                act.activation(rstd[:, :], rstd[:, :], ACT.Exp, scale=-0.5).then_inc(u_rstd, 1)

            def silus(u, j):
                s = 2 * u + j
                wait(act, k_yz, 2 * s - 2)
                for c in range(2):
                    t = slice(c * T, (c + 1) * T)
                    act.wait_ge(p_zc, 2 * s + c + 1)
                    act.activation(sz[:, j, t], sz[:, j, t], ACT.Silu)
                act.wait_ge(p_conv, 2 * s + 2)
                act.activation(xc[:, j, :], PS[:, 5:7, :].rearrange("p a t -> p (a t)"), ACT.Silu,
                               bias=c_bconv).then_inc(p_silu, 1)
                act.preload_act_table_set(EXP_LN)

            def dt_exp(u, j, c):
                t, k = slice(c * T, (c + 1) * T), 2 * (2 * u + j) + c + 1
                act.wait_ge(p_dtv, k)
                act.activation(vab[:, t], vab[:, t], ACT.Exp, bias=c_bdt).then_inc(p_e, 1)

            def dt_log(u, j, c):
                t, k = slice(c * T, (c + 1) * T), 2 * (2 * u + j) + c + 1
                act.wait_ge(p_rest, k)
                act.activation(wlog[:, t], wlog[:, t], ACT.Ln).then_inc(p_ln, 1)

            def bc_hi(u, j, c):
                t, k = slice(c * T, (c + 1) * T), 2 * (2 * u + j) + c + 1
                act.wait_ge(p_bc, k)
                act.activation(spl[:, j, t], PS[0:96, 5 + c, :], ACT.Copy).then_inc(p_h, 1)

            def bc_mid(u, j, c):
                t, k = slice(c * T, (c + 1) * T), 2 * (2 * u + j) + c + 1
                act.wait_ge(p_r, k)
                act.activation(spl[0:64, j, t], res3[:, t], ACT.Copy).then_inc(p_m, 1)

            def y_sq(u, j):
                act.wait_ge(p_ymc, 2 * u + j + 1)
                act.activation(ysq[:, :], ymc[:, :], ACT.Square).then_inc(p_ysq, 1)

            def y_rstd(u, j):
                s = 2 * u + j
                act.wait_ge(p_yvar, s + 1)
                act.activation(yrs[:, :], PS[:, 7, :], ACT.Ln, bias=c_eps).then_inc(p_yln, 1)
                act.wait_ge(p_yln, s + 1)
                act.activation(yrs[:, :], yrs[:, :], ACT.Exp, scale=-0.5).then_inc(p_yrs, 1)

            def gelus(u, j):
                s = 2 * u + j
                act.wait_ge(p_f1, 4 * s + 4)
                act.wait_ge(p_f1c, s + 1)
                for h, c, src in ((0, 0, gel[0][:, 0:T]), (0, 1, PS[:, 6, :]), (1, 0, PS[:, 7, :]), (1, 1, PS[:, 5, :])):
                    ins = act.activation(gel[h][:, c * T:(c + 1) * T], src, ACT.Gelu, bias=c_bf[:, h:h + 1])
                ins.then_inc(p_gel, 1)
                act.preload_act_table_set(EXP_LN)

            def skip_path(u, j):
                s = 2 * u + j
                act.wait_ge(u_xg, NJ * u + j + 1)
                wait(act, p_xi, s - 1)
                act.activation(xk[:, j, :], xhat[:, j, :], ACT.Identity, bias=c_kb[:, j:j + 1],
                               scale=c_skip).then_inc(p_xk, 1)

            def final(u):
                act.wait_ge(u_wout, u + 1)
                act.wait_ge(u_free, u + 1)
                for h in range(2):
                    ins = act.activation(fin[:, h, :], PS[:, 5 + h, :], ACT.Silu, bias=c_shift[:, h:h + 1],
                                         scale=c_scale[:, h:h + 1])
                ins.then_inc(u_fin, 1)
                act.preload_act_table_set(EXP_LN)

            def decays(u, q):
                g = u * (2 * NQ) + q
                n, c, j = q % NS, q // NS % 2, q // NQ
                if n == 0:
                    act.wait_ge(p_u, 2 * (2 * u + j) + c + 1)
                if not (isinstance(u, int) and u == 0 and q < DEEP):
                    act.wait_ge(q_scan, g - (DEEP - 1))
                act.activation(decay[:, q % DEEP, :], dt[:, j, c * T:(c + 1) * T], ACT.Exp,
                               scale=aneg[:, n:n + 1]).then_inc(q_exp, 1)

            def copy_c(u, q):
                g = u * (2 * NQ) + q
                act.wait_ge(q_c, g + 1)
                if not (isinstance(u, int) and u == 0 and q < RING):
                    act.wait_ge(q_prod, g - (RING - 1))
                act.activation(csb[:, q % RING, :], PS[:, 2 + q % 2, :], ACT.Copy).then_inc(q_cc, 1)

            front_steps.extend([silus, dt_exp, dt_log, bc_hi, bc_mid])

            def emit(u):
                for slot in range(2 * NQ):
                    for step, lead in ((decays, LEAD_EXP), (copy_c, LEAD_CC)):
                        du, q = split_slot(slot + lead)
                        if exists(u + du):
                            step(u + du, q)
                    for step, at, du in ((load_x, U_LOADX, 1), (norm_sq, U_SQ, 1), (norm_rstd, U_RSTD, 1),
                                         (final, U_FIN, -1)):
                        if slot == at and exists(u + du):
                            step(u + du)
                    for j in range(2):
                        if slot == U_SHIFT + j and exists(u + 1):
                            shift(u + 1, j)
                        for c in range(2):
                            run(u, slot, dt_exp, F_E + c, j, c)
                            run(u, slot, dt_log, F_LN + c, j, c)
                            run(u, slot, bc_hi, F_HI + c, j, c)
                            run(u, slot, bc_mid, F_MID + c, j, c)
                        run(u, slot, silus, F_SILU, j)
                        run(u, slot, y_sq, B_YSQ, j)
                        run(u, slot, y_rstd, B_YRSTD, j)
                        run(u, slot, gelus, B_GELU, j)
                        if slot == j * NQ + B_XK - NQ:
                            if exists(u):
                                skip_path(u, j)

            emit(-1)
            emit(0)
            with act.Fori(1, NU - 1) as u:
                emit(u)
            emit(NU - 1)
            emit(NU)

        @block.tensor
        def _(pe):
            pe.wait_ge(s_cst, 4)
            pe.wait_ge(s_w, 16 * (NW + 14))
            pe.matmul(PS[:, 4, 0:P], wxp[:, :], wdt[:, :], start=True, stop=True)
            for h in range(2):
                for c in range(2):
                    if c == 0:
                        ins = pe.matmul(PS[:, 5, h:h + 1], wfc1r[0:DM, h * P:(h + 1) * P], c_b1[0:DM, :],
                                        start=(h == 0), stop=True, skip_group_check=True)
            ins.then_inc(s_pp, 1)

            def gn_pe(n):
                pe.wait_ge(s_gp, n)
                pe.matmul(PS[:, 0, 0:NI], grp8[:, :], st[:, 0, :], start=True, stop=True).then_inc(s_pg, 1)
                pe.wait_ge(s_gp, n + 1)
                pe.matmul(PS[:, 1, 0:NI], grp8[:, :], st[:, 3, :], start=True, stop=True).then_inc(s_pg, 1)
            gn_pe(1)
            pe.wait_ge(s_gp, 3)
            for b in range(NB):
                for h in range(2):
                    for j in range(NJ):
                        i = b * 2 + h
                        ins = pe.matmul(PS[:, 2, i * KK:(i + 1) * KK],
                                        pooled[:, b * NJ + j, h * P:(h + 1) * P], wcT[:, j, :],
                                        start=(i == 0 and j == 0), stop=(j == NJ - 1), skip_group_check=True)
            ins.then_inc(s_pg, 1)
            pe.wait_ge(s_gp, 4)
            pe.matmul(PS[:, 3, 0:NI * KK], ones[:, :], sg[:, :, :].rearrange("p g o -> p (g o)"),
                      start=True, stop=True).then_inc(s_pg, 1)
            pe.wait_ge(s_gp, 5)
            pe.matmul(PS[:, 0, 0:NI * KK], ones[:, :], sq9[:, :, :].rearrange("p g o -> p (g o)"),
                      start=True, stop=True).then_inc(s_pg, 1)
            pe.sem_inc(s_taps, 2)
            with pe.Fori(0, NB) as b:
                for j in range(NJ):
                    pe.wait_ge(s_diag, b * NJ + (j + 1))
                    for k in range(NP):
                        n = b * (NJ * NP) + (j * NP + k)
                        pe.wait_ge(s_hat, n + 1)
                        pe.wait_ge(s_tapr, n + 1)
                        for rb in range(4):
                            for i, tap in enumerate(PE_TAPS):
                                dy, dx = tap // 3, tap % 3
                                ins = pe.matmul(PS[:, 4 * (k % 2) + rb, :].rearrange("p (r c) -> p r c", c=WW),
                                                dgw[:, j, i, :],
                                                xh[k % 2][:, 4 * rb + dy:4 * rb + dy + 4, dx:dx + WW],
                                                start=(i == 0), stop=(i == len(PE_TAPS) - 1))
                        ins.then_inc(s_taps, 1)
            gn_pe(6)
            pe.wait_ge(s_c, 1)
            pe.wait_ge(s_prep, 1)

            W = [PS[:, 5, :], PS[:, 6, :]]
            V = PS[:, 7, :]

            def norm_mean(u):
                pe.wait_ge(u_hat, u + 1)
                wait(pe, p_xi, 2 * u - 2)
                pe.matmul(V, mean256[:, :], xhat[:, 0, :], start=True, stop=False)
                pe.matmul(V, mean256[:, :], xhat[:, 1, :], start=False, stop=True).then_inc(u_mean, 1)

            def norm_var(u):
                pe.wait_ge(u_sq, u + 1)
                pe.matmul(V, mean256[:, :], sq[:, 0, :], start=True, stop=False)
                pe.matmul(V, mean256[:, :], sq[:, 1, :], start=False, stop=True).then_inc(u_var, 1)

            def proj_z(u, j, c):
                pe.wait_ge(u_xn, NJ * u + j + 1)
                if c == 0 and j == 0:
                    wait(pe, u_fin, u - 1)
                elif c == 0:
                    wait(pe, p_gel, 2 * u - 1)
                pe.matmul(W[c], win[c * DM:(c + 1) * DM, DI:], xn[c * DM:(c + 1) * DM, j, c, 3:],
                          start=True, stop=True).then_inc(p_z, 1)

            def conv(u, j, c, k):
                s = 2 * u + j
                if k == 0:
                    pe.wait_ge(p_zc, 2 * s + c + 1)
                    pe.wait_ge(u_shift[j], 32 * (u + 1))
                ins = pe.matmul(W[c], wconv[:, c, k, :], xn[:, j, c, 2 * k + 1:2 * k + 1 + T],
                                start=(k == 0), stop=(k == 1))
                if k == 1:
                    ins.then_inc(p_conv, 1)

            def proj_dt(u, j, c):
                pe.wait_ge(p_silu, 2 * u + j + 1)
                pe.matmul(W[c], wdx[:, :], xc[:, j, c * T:(c + 1) * T], start=True, stop=True).then_inc(p_dt, 1)

            def proj_bc(u, j, c):
                pe.wait_ge(p_dtv, 2 * (2 * u + j) + c + 1)
                pe.matmul(PS[0:96, 5 + c, :], wbc[:, :], xc[:, j, c * T:(c + 1) * T],
                          start=True, stop=True).then_inc(p_bc, 1)

            def out_proj(u, j):
                s = 2 * u + j
                pe.wait_ge(k_yz, 2 * s + 2)
                wait(pe, p_xi, s)
                if j == 0 and exists(u + 1) and not (isinstance(u, int) and u == NU - 1):
                    pe.wait_ge(u_ln, u + 2)
                for c in range(2):
                    ins = pe.matmul(PS[c * DM:(c + 1) * DM, 7, :], wop[:, :], yz[:, c, :], start=True, stop=True)
                ins.then_inc(p_op, 1)

            def y_var(u, j):
                pe.wait_ge(p_ysq, 2 * u + j + 1)
                pe.matmul(V, half64[:, :], ysq[:, :], start=True, stop=True).then_inc(p_yvar, 1)

            def fc1(u, j, i):
                s = 2 * u + j
                h, c, bank = ((0, 0, 5), (0, 1, 6), (1, 0, 7), (1, 1, 5))[i]
                if i == 0:
                    pe.wait_ge(p_yn, s + 1)
                if i < 2:
                    if s_is_front(u, j):
                        pe.wait_ge(p_r, 2 * (s + 2) + i + 1)
                    elif j == 0:
                        pe.wait_ge(u_fin, u)
                    if j == 0:
                        wait(pe, u_fin, u)
                if i == 3:
                    pe.wait_ge(p_f1c, s + 1)
                pe.matmul(PS[:, bank, :], wfc1[c * DM:(c + 1) * DM, h * P:(h + 1) * P], yn[c * DM:(c + 1) * DM, :],
                          start=True, stop=True).then_inc(p_f1, 1)

            def s_is_front(u, j):
                return not (isinstance(u, int) and u == NU - 1)

            def fc2(u, j):
                pe.wait_ge(p_gel, 2 * u + j + 1)
                for h in range(2):
                    for c in range(2):
                        ins = pe.matmul(PS[c * DM:(c + 1) * DM, 7, :], wfc2[:, h, :], gel[h][:, c * T:(c + 1) * T],
                                        start=(h == 0), stop=(h == 1))
                ins.then_inc(p_f2, 1)

            def w_out(u, h):
                pe.wait_ge(p_xi, 2 * u + 2)
                for j in range(NJ):
                    ins = pe.matmul(W[h], wout[:, j, h * P:(h + 1) * P], xi[:, j, :],
                                    start=(j == 0), stop=(j == NJ - 1))
                if h == 1:
                    ins.then_inc(u_wout, 1)

            def bcast(u, q, bank, row, count, copied):
                g = u * (2 * NQ) + q
                n, c, j = q % NS, q // NS % 2, q // NQ
                if n == 0:
                    pe.wait_ge(p_l, 2 * (2 * u + j) + c + 1)
                if not (isinstance(u, int) and u == 0 and q < 2):
                    pe.wait_ge(copied, g - 1)
                pe.matmul(PS[:, bank + q % 2, :], sel[:, row + n, :], spl[:, j, c * T:(c + 1) * T],
                          start=True, stop=True).then_inc(count, 1)

            def total(u, q):
                n, c, j = q % NS, q // NS % 2, q // NQ
                chunk = (2 * u + j) * 2 + c
                if n + 1 in ADDED:
                    return
                if n in ADDED:
                    pe.wait_ge(q_add, chunk * len(ADDED) + ADDED.index(n) + 1)
                else:
                    pe.wait_ge(q_prod, u * (2 * NQ) + q + 1)
                if n == 0:
                    wait(pe, k_y, chunk)
                pe.matmul(PS[:, 4, :], ident[:, :], prod[:, q % DEEP, :], start=(n == 0),
                          stop=(n == NS - 1), skip_group_check=True).then_inc(q_sum, 2 if n in ADDED else 1)

            front_steps.extend([proj_z, conv, proj_dt, proj_bc])
            conv_k = [lambda u, j, c, k=k: conv(u, j, c, k) for k in range(2)]
            fc1_i = [lambda u, j, i=i: fc1(u, j, i) for i in range(4)]
            front_steps.extend(conv_k)

            def emit(u):
                for slot in range(2 * NQ):
                    du, q = split_slot(slot + LEAD_B)
                    if exists(u + du):
                        bcast(u + du, q, 0, 0, q_b, q_drv)
                    du, q = split_slot(slot + LEAD_C)
                    if exists(u + du):
                        bcast(u + du, q, 2, NS, q_c, q_cc)
                    if slot == U_MEAN and exists(u + 1):
                        norm_mean(u + 1)
                    if slot == U_VAR and exists(u + 1):
                        norm_var(u + 1)
                    for h in range(2):
                        if slot == U_WOUT + h and exists(u - 1):
                            w_out(u - 1, h)
                    for j in range(2):
                        run(u, slot, out_proj, B_OUTP, j)
                        run(u, slot, y_var, B_YVAR, j)
                        for c in range(2):
                            run(u, slot, proj_z, F_Z + c, j, c)
                            for k in range(2):
                                run(u, slot, conv_k[k], F_CONV + 2 * c + k, j, c)
                            run(u, slot, proj_dt, F_DT + c, j, c)
                            run(u, slot, proj_bc, F_BC + c, j, c)
                        for i in range(4):
                            run(u, slot, fc1_i[i], B_FC1 + (i + 1) // 2, j)
                        run(u, slot, fc2, B_FC2, j)
                    du, q = split_slot(slot - LAG)
                    if exists(u + du):
                        total(u + du, q)

            emit(-1)
            emit(0)
            with pe.Fori(1, NU - 1) as u:
                emit(u)
            emit(NU - 1)
            emit(NU)

        @block.vector
        def _(dve):
            steps = [0]

            def link(ins):
                steps[0] += 1
                ins.then_inc(s_dv, 1)
                dve.wait_ge(s_dv, steps[0])

            link(dve.memset(c_eps, EPS))
            link(dve.memset(c_one, 1.0))
            link(dve.memset(init[:, :], 0.0))
            link(dve.memset(xn[:, :, :, 0:3], 0.0))
            dve.sem_inc(s_aused, 4)
            with dve.Fori(0, NI) as im:
                for k in range(NP):
                    dve.wait_ge(s_aload[k % 4], im * (16 * NP // 4) + 16 * (k // 4 + 1))
                    for rb in range(2):
                        dve.tensor_reduce(pooled[:, bass.ds(im, 1), k * 32 + 16 * rb:k * 32 + 16 * rb + 16].rearrange(
                                              "p a w -> p (a w)"),
                                          xa[k % 4][:, rb * 1024:(rb + 1) * 1024].rearrange("p (r w c) -> p w r c", r=8, c=8),
                                          AX.XY, ALU.add)
                    for i in range(4):
                        ins = dve.bn_stats(bnst[:, k * 4 + i, :], xa[k % 4][:, i * 512:(i + 1) * 512])
                    ins.then_inc(s_aused, 1)
                dve.wait_ge(s_aused, im * NP + (NP + 4))
                dve.sem_inc(s_bst, 1)
                dve.bn_aggr(mvt[:, :], bnst[:, :, :]).then_inc(s_bst, 1)
                dve.wait_ge(s_bst, im * 2 + 2)
                dve.tensor_copy(mv[:, bass.ds(im, 1), :].rearrange("p a k -> p (a k)"), mvt[:, :]).then_inc(s_mv, 1)
            dve.wait_ge(s_mv, NI)

            def gn_dve(n_gp, n_pg, n_ga):
                link(dve.tensor_copy(st[:, 0, :], mv[:, :, 0]))
                dve.sem_inc(s_gp, 1)
                dve.wait_ge(s_pg, n_pg)
                link(dve.tensor_copy(st[:, 1, :], PS[:, 0, 0:NI]))
                link(dve.tensor_tensor(st[:, 2, :], st[:, 0, :], st[:, 1, :], ALU.subtract))
                link(dve.tensor_tensor(st[:, 2, :], st[:, 2, :], st[:, 2, :], ALU.mult))
                link(dve.tensor_tensor(st[:, 3, :], st[:, 2, :], mv[:, :, 1], ALU.add))
                dve.sem_inc(s_gp, 1)
                dve.wait_ge(s_pg, n_pg + 1)
                link(dve.tensor_scalar(st[:, 4, :], PS[:, 1, 0:NI], EPS, None, ALU.add))
                dve.sem_inc(s_ga, 1)
                dve.wait_ge(s_ag, n_ga)
                link(dve.reciprocal(coef[:, 0, :], st[:, 5, :]))
                link(dve.scalar_tensor_tensor(out=coef[:, 1, :], in0=st[:, 1, :], scalar=-1.0, in1=coef[:, 0, :],
                                              op0=ALU.mult, op1=ALU.mult))

            link(dve.memset(st[:, 6, :], 0.0))
            gn_dve(1, 1, 1)
            link(dve.tensor_scalar(st[:, 7, :], coef[:, 0, :], 1 / 64, None, ALU.mult))
            for i in range(NI):
                link(dve.tensor_scalar(pooled[:, i, :], pooled[:, i, :], st[:, 7, i:i + 1], coef[:, 1, i:i + 1],
                                       ALU.mult, ALU.add))
            dve.sem_inc(s_gp, 1)
            dve.wait_ge(s_pg, 3)
            link(dve.tensor_copy(sg[:, :, :], PS[:, 2, 0:NI * KK].rearrange("p (g o) -> p g o", o=KK)))
            dve.sem_inc(s_gp, 1)
            dve.wait_ge(s_pg, 4)
            link(dve.tensor_reduce(s9[:, 0, :], PS[:, 3, 0:NI * KK].rearrange("p (g o) -> p o g", o=KK), AX.X, ALU.add))
            link(dve.tensor_scalar(s9[:, 0, :], s9[:, 0, :], 1 / (NI * P), None, ALU.mult))
            for i in range(NI):
                link(dve.tensor_tensor(sgd[:, i, :], sg[:, i, :], s9[:, 0, :], ALU.subtract))
            link(dve.tensor_tensor(sq9[:, :, :], sgd[:, :, :], sgd[:, :, :], ALU.mult))
            dve.sem_inc(s_gp, 1)
            dve.wait_ge(s_pg, 5)
            link(dve.tensor_reduce(s9[:, 1, :], PS[:, 0, 0:NI * KK].rearrange("p (g o) -> p o g", o=KK), AX.X, ALU.add))
            link(dve.tensor_scalar(s9[:, 1, :], s9[:, 1, :], 1 / (NI * P), EPS, ALU.mult, ALU.add))
            dve.sem_inc(s_ga, 1)
            dve.wait_ge(s_ag, 2)
            link(dve.reciprocal(s9[:, 3, :], s9[:, 2, :]))
            dve.wait_ge(s_w, 16 * (NW + 14))
            link(dve.tensor_tensor(s9[:, 3, :], s9[:, 3, :], gam[:, :], ALU.mult))
            for i in range(NI):
                v = w9[:, i * KK:(i + 1) * KK]
                link(dve.tensor_tensor(v, sgd[:, i, :], s9[:, 3, :], ALU.mult))
                link(dve.tensor_tensor(v, v, bet[:, :], ALU.add))
            for k in range(KC // 2):
                for c in range(2):
                    for half in range(2):
                        rows = slice(half * DM, half * DM + DM)
                        tap = 2 * k + (1 if half == c else 0)
                        link(dve.tensor_tensor(wconv[rows, c, k, :], win[rows, 0:DI], cvr[rows, tap, :], ALU.mult))
            for j in range(NJ):
                link(dve.scalar_tensor_tensor(out=c_kb[:, j:j + 1], in0=c_bn[:, j:j + 1], scalar=c_skip, in1=c_b2,
                                              op0=ALU.mult, op1=ALU.add))
            dve.wait_ge(s_pp, 1)
            link(dve.tensor_copy(wdx[:, :], PS[:, 4, 0:P]))
            link(dve.tensor_tensor(c_bf, PS[:, 5, 0:2], c_bfc1, ALU.add))
            link(dve.tensor_reduce(wsum[:, :], wop[:, :], AX.X, ALU.add))
            link(dve.tensor_scalar(wsum[:, :], wsum[:, :], 1 / DM, None, ALU.mult))
            link(dve.tensor_scalar(wop[:, :], wop[:, :], wsum[:, 0:1], None, ALU.subtract))
            link(dve.tensor_scalar(wfc1[:, :], wfc1r[:, :], c_g1, None, ALU.mult))
            dve.wait_ge(s_an, 1)
            link(dve.tensor_scalar(aneg[:, :], aneg[:, :], -1.0, None, ALU.mult))
            link(dve.tensor_scalar(c_scale, c_bnv, EPS, None, ALU.add))
            dve.sem_inc(s_ga, 1)
            dve.wait_ge(s_ag, 3)
            link(dve.reciprocal(c_tmp, c_tmp))
            link(dve.tensor_tensor(c_scale, c_tmp, c_bng, ALU.mult))
            link(dve.tensor_tensor(c_tmp, c_scale, c_bnm, ALU.mult))
            link(dve.tensor_tensor(c_shift, c_bnb, c_tmp, ALU.subtract))
            dve.sem_inc(s_prep, 1)
            dve.wait_ge(s_cst, 4)
            for i in range(2):
                for col in (0, 129):
                    link(dve.memset(xh[i][:, :, col:col + 1], 0.0))
            dve.sem_inc(s_ga, 1)
            dve.sem_inc(s_bused, 2)
            dve.sem_inc(s_htap, 2)
            dve.sem_inc(s_tapr, 2)
            dve.sem_inc(s_x1free, 2)
            base = steps[0]
            per = NJ * (NP * (1 + len(DVE_TAPS)) + 2)
            with dve.Fori(0, NB) as b:
                done = [0]

                def link_b(ins):
                    done[0] += 1
                    ins.then_inc(s_dv, 1)
                    dve.wait_ge(s_dv, b * per + (base + done[0]))
                for j in range(NJ):
                    w0 = (b * NJ + j) * KK
                    dve.wait_ge(s_taps, b * (NJ * NP) + (j * NP - NP + 2) if j else b * (NJ * NP) + 2)
                    for i, tap in enumerate(PE_TAPS):
                        ins = dve.tensor_scalar(dgw[:, j, i, :], ident[:, :], w9[:, bass.ds(w0 + tap, 1)], None, ALU.mult)
                    ins.then_inc(s_diag, 1)
                    for k in range(NP):
                        n = b * (NJ * NP) + (j * NP + k)
                        acc = x1t[k % 2].rearrange("p (r c) -> p r c", c=WW)
                        dve.wait_ge(s_taps, n + 3)
                        dve.wait_ge(s_x1free, n + 1)
                        link_b(dve.tensor_tensor(acc, xb[k % 2][:, 1:17, :],
                                                 PS[:, 4 * (k % 2):4 * (k % 2) + 4, :].rearrange(
                                                     "p a (r c) -> p (a r) c", c=WW), ALU.add))
                        dve.sem_inc(s_bused, 1)
                        dve.sem_inc(s_tapr, 1)
                        for tap in DVE_TAPS:
                            dy, dx = tap // 3, tap % 3
                            link_b(dve.scalar_tensor_tensor(out=acc, in0=xh[k % 2][:, dy:dy + PR, dx:dx + WW],
                                                            scalar=w9[:, bass.ds(w0 + tap, 1)], in1=acc,
                                                            op0=ALU.mult, op1=ALU.add))
                        dve.sem_inc(s_htap, 1)
                        dve.sem_inc(s_x1, 1)
                        for i in range(4):
                            ins = dve.bn_stats(bnst[:, k * 4 + i, :], x1t[k % 2][:, i * 512:(i + 1) * 512])
                    link_b(ins)
                    dve.sem_inc(s_bst, 1)
                    link_b(dve.bn_aggr(mvt[:, :], bnst[:, :, :]))
                    dve.tensor_copy(mv[:, bass.ds(b * NJ + j, 1), :].rearrange("p a k -> p (a k)"), mvt[:, :]).then_inc(s_mv, 1)
            dve.wait_ge(s_mv, 2 * NI)
            steps[0] = base + NB * per
            gn_dve(6, 6, 4)
            for b in range(NB):
                for i in range(2):
                    link(dve.tensor_copy(coefU[:, b * UPB:(b + 1) * UPB, 2 * i:2 * i + 2],
                                         coef[:, i:i + 1, b * NJ:(b + 1) * NJ].to_broadcast([P, UPB, NJ])))
            dve.sem_inc(s_coef, 1)
            dve.wait_ge(s_c, 1)
            dve.sem_inc(u_res, 1)
            dve.sem_inc(u_free, 1)

            def norm_hat(u):
                dve.wait_ge(u_xl, (u + 1) * 16)
                wait(dve, p_xk, 2 * u)
                for j in range(NJ):
                    ins = dve.tensor_scalar(xhat[:, j, :], xl[:, j * T:(j + 1) * T],
                                            coefU[:, bass.ds(u, 1), j:j + 1].rearrange("p a k -> p (a k)"),
                                            coefU[:, bass.ds(u, 1), 2 + j:3 + j].rearrange("p a k -> p (a k)"),
                                            ALU.mult, ALU.add)
                ins.then_inc(u_hat, 1)

            def norm_centre(u):
                dve.wait_ge(u_mean, u + 1)
                for j in range(NJ):
                    ins = dve.tensor_tensor(xhat[:, j, :], xhat[:, j, :], PS[:, 7, :], ALU.subtract)
                ins.then_inc(u_cen, 1)

            def norm_out(u, j):
                own = [xn[c * DM:(c + 1) * DM, j, c, :] for c in range(2)]
                if not (isinstance(u, int) and u == 0):
                    dve.wait_ge(u_shift[j], 32 * u)
                    dve.sem_inc(u_hist, 1)
                    for c in range(2):
                        ins = dve.tensor_scalar(own[c][:, 0:3], own[c][:, T:T + 3],
                                                keep[c * DM:(c + 1) * DM, bass.ds(u - 1, 1)], None, ALU.mult)
                    ins.then_inc(u_hist, 1)
                    dve.wait_ge(u_hist, 2 * (NJ * (u - 1) + j + 1))
                dve.wait_ge(u_rstd, u + 1)
                dve.scalar_tensor_tensor(out=xhat[:, j, :], in0=xhat[:, j, :], scalar=c_gn[:, j:j + 1],
                                         in1=rstd[:, :], op0=ALU.mult, op1=ALU.mult).then_inc(u_xg, 1)
                dve.wait_ge(u_xg, NJ * u + j + 1)
                for c in range(2):
                    ins = dve.tensor_scalar(own[c][:, 3:], xhat[c * DM:(c + 1) * DM, j, :],
                                            c_bn[c * DM:(c + 1) * DM, j:j + 1], None, ALU.add)
                ins.then_inc(u_xn, 1)

            def count(u, j, c):
                return 2 * (2 * u + j) + c + 1

            def z_copy(u, j, c):
                dve.wait_ge(p_z, count(u, j, c))
                dve.tensor_copy(sz[:, j, c * T:(c + 1) * T], PS[:, 5 + c, :]).then_inc(p_zc, 1)

            def dt_read(u, j, c):
                t = slice(c * T, (c + 1) * T)
                dve.wait_ge(p_dt, count(u, j, c))
                dve.tensor_scalar(rlu[:, t], PS[:, 5 + c, :], c_bdt, 0.0, ALU.add, ALU.max).then_inc(p_rl, 1)
                dve.wait_ge(p_rl, count(u, j, c))
                dve.scalar_tensor_tensor(out=vab[:, t], in0=rlu[:, t], scalar=-2.0, in1=PS[:, 5 + c, :],
                                         op0=ALU.mult, op1=ALU.add).then_inc(p_dtv, 1)

            def dt_rest(u, j, c):
                t = slice(c * T, (c + 1) * T)
                dve.wait_ge(p_e, count(u, j, c))
                dve.tensor_scalar(wlog[:, t], vab[:, t], 1.0, None, ALU.add).then_inc(p_w, 1)
                dve.wait_ge(p_w, count(u, j, c))
                wait(dve, p_dtin, count(u, j, c) - 2)
                dve.scalar_tensor_tensor(out=wrest[:, t], in0=wlog[:, t], scalar=-1.0, in1=vab[:, t],
                                         op0=ALU.add, op1=ALU.subtract).then_inc(p_rest, 1)

            def dt_sum(u, j, c):
                t = slice(c * T, (c + 1) * T)
                dve.wait_ge(p_ln, count(u, j, c))
                dve.wait_ge(p_dtin, count(u, j, c))
                dve.tensor_tensor(dt[:, j, t], wlog[:, t], rlu[:, t], ALU.add).then_inc(p_dts, 1)
                dve.wait_ge(p_dts, count(u, j, c))
                dve.tensor_tensor(du[:, j, t], dt[:, j, t], xc[:, j, t], ALU.mult).then_inc(p_u, 1)

            def bc_rest(u, j, c):
                t = slice(c * T, (c + 1) * T)
                dve.wait_ge(p_h, count(u, j, c))
                dve.tensor_tensor(res3[:, t], PS[0:64, 5 + c, :], spl[0:64, j, t], ALU.subtract).then_inc(p_r, 1)

            def bc_low(u, j, c):
                t = slice(c * T, (c + 1) * T)
                dve.wait_ge(p_m, count(u, j, c))
                dve.tensor_tensor(spl[0:32, j, t], res3[0:32, t], spl[0:32, j, t], ALU.subtract).then_inc(p_l, 1)

            def y_copy(u, j):
                dve.wait_ge(p_op, 2 * u + j + 1)
                dve.tensor_copy(ymc[:, :], PS[:, 7, :]).then_inc(p_ymc, 1)

            def y_norm(u, j):
                dve.wait_ge(p_yrs, 2 * u + j + 1)
                dve.tensor_tensor(yn[:, :], ymc[:, :], yrs[:, :], ALU.mult).then_inc(p_yn, 1)

            def fc1_copy(u, j):
                dve.wait_ge(p_f1, 4 * (2 * u + j) + 1)
                dve.tensor_copy(gel[0][:, 0:T], PS[:, 5, :]).then_inc(p_f1c, 1)

            def mix_in(u, j):
                s = 2 * u + j
                dve.wait_ge(p_f2, s + 1)
                dve.wait_ge(p_xk, s + 1)
                dve.tensor_tensor(xi[:, j, :], PS[:, 7, :], xk[:, j, :], ALU.add).then_inc(p_xi, 1)

            def result(u):
                dve.wait_ge(u_fin, u + 1)
                dve.wait_ge(u_xr, (u + 1) * 16)
                fo = fin[:, :, :].rearrange("p j t -> p (j t)")
                dve.tensor_tensor(fo, xres, fo, ALU.add).then_inc(u_res, 1)

            def drive_q(u, q):
                c, j = q // NS % 2, q // NQ
                dve.wait_ge(q_b, u * (2 * NQ) + q + 1)
                dve.tensor_tensor(drive[:, q % RING, :], du[:, j, c * T:(c + 1) * T], PS[:, q % 2, :],
                                  ALU.mult).then_inc(q_drv, 1)

            def scan_q(u, q):
                g = u * (2 * NQ) + q
                dve.wait_ge(q_drv, g + 1)
                dve.wait_ge(q_exp, g + 1)
                if not (isinstance(u, int) and u == 0 and q < DEEP):
                    dve.wait_ge(q_prod, g - (DEEP - 1))
                dve.tensor_tensor_scan(hst[:, q % DEEP, :], decay[:, q % DEEP, :], drive[:, q % RING, :],
                                       init[:, q:q + 1], ALU.mult, ALU.add).then_inc(q_scan, 1)

            def y_end(u, j, c):
                s = 2 * u + j
                dve.wait_ge(q_sum, s * NQ + (c + 1) * NS)
                dve.scalar_tensor_tensor(out=ytmp[:, :], in0=xc[:, j, c * T:(c + 1) * T], scalar=c_D,
                                         in1=PS[:, 4, :], op0=ALU.mult, op1=ALU.add).then_inc(k_y, 1)
                dve.wait_ge(k_y, s * 2 + (c + 1))
                wait(dve, p_op, s)
                dve.tensor_tensor(yz[:, c, :], ytmp[:, :], sz[:, j, c * T:(c + 1) * T], ALU.mult).then_inc(k_yz, 1)

            front_steps.extend([z_copy, dt_read, dt_rest, dt_sum, bc_rest, bc_low])

            def emit(u):
                for slot in range(2 * NQ):
                    du_, q = split_slot(slot + LEAD_DRV)
                    if exists(u + du_):
                        drive_q(u + du_, q)
                    if exists(u):
                        scan_q(u, slot)
                    for c in range(4):
                        du_, q = split_slot(NS * (c + 1) + LAG)
                        if slot == q and exists(u - du_):
                            y_end(u - du_, c // 2, c % 2)
                    if slot == U_HAT and exists(u + 1):
                        norm_hat(u + 1)
                    if slot == U_CEN and exists(u + 1):
                        norm_centre(u + 1)
                    for j in range(NJ):
                        if slot == U_XN + j and exists(u + 1):
                            norm_out(u + 1, j)
                    if slot == U_RES and exists(u - 1):
                        result(u - 1)
                    for j in range(2):
                        run(u, slot, y_copy, B_YMC, j)
                        run(u, slot, y_norm, B_YN, j)
                        run(u, slot, fc1_copy, B_FC1C, j)
                        run(u, slot, mix_in, B_XI, j)
                        for c in range(2):
                            run(u, slot, z_copy, F_ZC + c, j, c)
                            run(u, slot, dt_read, F_DTV + c, j, c)
                            run(u, slot, dt_rest, F_W + c, j, c)
                            run(u, slot, bc_rest, F_RES + c, j, c)
                            run(u, slot, bc_low, F_LO + c, j, c)
                            run(u, slot, dt_sum, F_DTU + c, j, c)

            emit(-1)
            emit(0)
            with dve.Fori(1, NU - 1) as u:
                emit(u)
            emit(NU - 1)
            emit(NU)


def kernel(**inputs):
    import numpy as _np
    import concourse.bacc as _bacc
    from concourse import mybir as _mybir
    from concourse.bass_utils import run_bass_kernel_spmd as _run

    nc = _bacc.Bacc("TRN2", target_bir_lowering=False, num_devices=1)
    i = {k.replace("L0_conv_", "L0").replace("L1_conv_", ""): _np.asarray(v) for k, v in inputs.items()}
    arranged = [
        ("x", i["x"]), ("w_conv", i["L0w_conv"].T), ("gamma", i["L0gamma"]), ("beta", i["L0beta"]),
        ("g_norm", i["g_norm"]), ("b_norm", i["b_norm"]), ("g_norm1", i["g_norm1"]), ("b_norm1", i["b_norm1"]),
        ("W_inT", i["W_in"].T), ("W_cv", i["W_conv"].reshape(DI, KC).T.reshape(-1)), ("b_conv", i["b_conv"]),
        ("W_xp", i["W_xproj"]), ("W_xpT", i["W_xproj"].T), ("W_dtT", i["W_dt"].T), ("b_dt", i["b_dt"]),
        ("A_log", i["A_log"]), ("D_par", i["D_par"]), ("W_outpT", i["W_outp"].T), ("skip", i["skip_scale"]),
        ("W_fc1T", i["W_fc1"].T), ("b_fc1", i["b_fc1"]), ("W_fc2T", i["W_fc2"].T), ("b_fc2", i["b_fc2"]),
        ("W_outT", i["W_out"].T.reshape(DM, 4, CH).transpose(1, 0, 2).reshape(CH, CH)), ("bn_g", i["bn_g"]), ("bn_b", i["bn_b"]), ("bn_m", i["bn_mean"]),
        ("bn_v", i["bn_var"]),
    ]
    arrays, args = {}, []
    for name, a in arranged:
        a = _np.ascontiguousarray(a)
        arrays[f"in_{name}"] = a
        args.append(nc.dram_tensor(f"in_{name}", a.shape, _mybir.dt.from_np(a.dtype), kind="ExternalInput").ap())
    args.append(nc.dram_tensor("out_y", (NB, CH, HH, WW), _mybir.dt.float32, kind="ExternalOutput").ap())
    build(nc, *args)
    r = _run(nc, [arrays], core_ids=[0])
    return r.results[0]["out_y"]
```
